# Optimizing a Trainium2 kernel written in Bass

```python
import numpy as np
import jax
import jax.numpy as jnp

def _softmax(x, axis=-1):
    return jax.nn.softmax(x, axis=axis)

def _gelu(x):
    return jax.nn.gelu(x, approximate=True)

def _silu(x):
    return jax.nn.silu(x)

def _sigmoid(x):
    return jax.nn.sigmoid(x)

def _layernorm(x, axis=-1, eps=1e-05):
    m = jnp.mean(x, axis=axis, keepdims=True)
    v = jnp.var(x, axis=axis, keepdims=True)
    return (x - m) / jnp.sqrt(v + eps)

def _scatter_add(tgt, idx, src, axis=0):
    return tgt.at[idx].add(src)

def _segment_sum(src, seg, n):
    return jax.ops.segment_sum(src, seg, n)
kernel_name = 'mk_flamingo_gated_d1_seqx_r8_9c2447'

def setup_inputs(seed: int=0):
    np.random.seed(seed)
    _w = jnp.asarray

    def _rec_inputs():
        import jax
        import jax.numpy as jnp
        _rk = jax.random.key(seed)
        x = 7.22e-05 + 1 * jax.random.normal(jax.random.fold_in(_rk, 1), (8, 256, 128), jnp.float32)
        _lenS = 256 - jax.random.randint(jax.random.fold_in(_rk, 7), (8,), 0, max(1, 256 // 4) + 1, jnp.int32)
        _lenS2 = 256 - jax.random.randint(jax.random.fold_in(_rk, 8), (8,), 0, max(1, 256 // 4) + 1, jnp.int32)
        _ctx_1024P = jax.random.normal(jax.random.fold_in(_rk, 11), (8, 16, 128), jnp.float32)
        _ctx_1024c = jax.random.dirichlet(jax.random.fold_in(_rk, 511), 0.3 * jnp.ones((16,), jnp.float32), (8, 256))
        _ctx_1024t = jnp.einsum('bsk,bkd->bsd', _ctx_1024c, _ctx_1024P)
        _ctx_1024t = _ctx_1024t * jax.lax.rsqrt(jnp.mean(jnp.square(_ctx_1024t)) + 1e-12) * 0.953939
        ctx_1024 = 0.00191187 + 0.999416 * (_ctx_1024t + 0.3 * jax.random.normal(jax.random.fold_in(_rk, 611), (8, 256, 128), jnp.float32))
        _g = jax.random.normal(jax.random.fold_in(_rk, 9001), (2, 1), jnp.float32)
        _g = jnp.sign(_g) * jnp.maximum(jnp.abs(_g), 1.0) + (_g == 0) * 1.0
        g_xattn = _g[0]
        g_ffn = _g[1]
        return (x, ctx_1024, g_xattn, g_ffn)
    x, ctx_1024, g_xattn, g_ffn = _rec_inputs()

    def _L0_xattn_setup():
        import jax, jax.numpy as jnp
        import numpy as np
        EPS = 1e-06

        def _rmsnorm(x, w, eps=EPS):
            x32 = x.astype(jnp.float32)
            var = jnp.mean(x32 * x32, axis=-1, keepdims=True)
            return (x32 * jax.lax.rsqrt(var + eps)).astype(x.dtype) * w
        key = jax.random.key(seed)
        ks = jax.random.split(key, 6)
        B, S, K, H = (4, 256, 64, 128)
        return {'hidden_states': jax.random.normal(ks[0], (B, S, H), jnp.float32), 'memory_state': jax.random.normal(ks[1], (B, K, H), jnp.float32), 'q_w': jax.random.normal(ks[2], (H, H), jnp.float32) * (1.0 / np.sqrt(H)), 'k_w': jax.random.normal(ks[3], (H, H), jnp.float32) * (1.0 / np.sqrt(H)), 'norm_w': jnp.ones((H,), jnp.float32), 'gate_w': jax.random.normal(ks[4], (H, H), jnp.float32) * 0.02, 'gate_b': jnp.zeros((H,), jnp.float32)}
    _L0_xattn_all = _L0_xattn_setup()
    _L0_xattn_in = {k: v for k, v in _L0_xattn_all.items() if k in ('q_w', 'k_w', 'norm_w', 'gate_w', 'gate_b')}
    del _L0_xattn_all

    def _L0_ffn_setup():
        import jax, jax.numpy as jnp
        import numpy as np
        B, T, C = (2, 256, 128)
        H, D = (16, 64)
        CR = 8
        R = C // CR
        ROPE = D // 2
        NOPE = D - ROPE
        E, K, I, S = (8, 2, 64, 1)
        THETA = 100000.0
        EPS = 1e-05

        def _rmsnorm(x, w):
            rms = jnp.sqrt(jnp.mean(x * x, axis=-1, keepdims=True) + EPS)
            return w * (x / rms)

        def _rope(xh):
            d = xh.shape[-1]
            t = jnp.arange(xh.shape[2], dtype=jnp.float32)
            freqs = 1.0 / THETA ** (jnp.arange(0, d, 2, dtype=jnp.float32) / d)
            ang = jnp.outer(t, freqs)
            cos, sin = (jnp.cos(ang), jnp.sin(ang))
            xr = xh.reshape(xh.shape[:-1] + (d // 2, 2))
            x0, x1 = (xr[..., 0], xr[..., 1])
            rot = jnp.stack([x0 * cos - x1 * sin, x0 * sin + x1 * cos], axis=-1)
            return rot.reshape(xh.shape)

        def _attention(x, Wq, Wkva, Wkvb, Wo):
            b, t, _ = x.shape
            q = (x @ Wq).reshape(b, t, H, D).transpose(0, 2, 1, 3)
            ckv = x @ Wkva
            kv_latent, k_rope = (ckv[:, :, :R], ckv[:, :, R:])
            kv = (kv_latent @ Wkvb).reshape(b, t, H, NOPE).transpose(0, 2, 1, 3)
            k_rope = jnp.broadcast_to(k_rope[:, None, :, :], (b, H, t, ROPE))
            q_nope, q_rope = (q[..., :NOPE], q[..., NOPE:])
            q = jnp.concatenate([q_nope, _rope(q_rope)], axis=-1)
            k = jnp.concatenate([kv, _rope(k_rope)], axis=-1)
            v = jnp.concatenate([kv, jnp.zeros_like(k_rope)], axis=-1)
            att = jnp.einsum('bhqd,bhkd->bhqk', q, k) / jnp.sqrt(jnp.float32(D))
            mask = jnp.tril(jnp.ones((t, t), dtype=bool))
            att = jnp.where(mask, att, jnp.float32(-jnp.inf))
            att = jax.nn.softmax(att, axis=-1)
            y = jnp.einsum('bhqk,bhkd->bhqd', att, v)
            y = y.transpose(0, 2, 1, 3).reshape(b, t, H * D)
            return y @ Wo

        def _experts(x_flat, Wg, Wu, Wd):
            g = jax.nn.silu(jnp.einsum('nc,eci->nei', x_flat, Wg))
            u = jnp.einsum('nc,eci->nei', x_flat, Wu)
            return jnp.einsum('nei,eic->nec', g * u, Wd)

        def _moe(x, Wgate, expert_bias, Wg, Wu, Wd, sWg, sWu, sWd):
            b, t, c = x.shape
            xf = x.reshape(-1, c)
            shared = jnp.mean(_experts(xf, sWg, sWu, sWd), axis=1)
            logits = xf @ Wgate + expert_bias
            probs = jax.nn.softmax(logits, axis=-1)
            topk_p, topk_i = jax.lax.top_k(probs, K)
            topk_p = topk_p / jnp.sum(topk_p, axis=-1, keepdims=True)
            comb = jnp.sum(jax.nn.one_hot(topk_i, E, dtype=xf.dtype) * topk_p[..., None], axis=1)
            routed = jnp.einsum('ne,nec->nc', comb, _experts(xf, Wg, Wu, Wd))
            return (shared + routed).reshape(b, t, c)
        key = jax.random.key(seed)
        ks = jax.random.split(key, 16)
        w = lambda k, shp: jax.random.normal(k, shp, dtype=jnp.float32) * 0.02
        return {'x': jax.random.normal(ks[0], (B, T, C), dtype=jnp.float32), 'w_ln1': jnp.ones((C,), jnp.float32), 'Wq': w(ks[1], (C, H * D)), 'Wkva': w(ks[2], (C, R + ROPE)), 'Wkvb': w(ks[3], (R, H * NOPE)), 'Wo': w(ks[4], (H * D, C)), 'w_ln2': jnp.ones((C,), jnp.float32), 'Wgate': w(ks[5], (C, E)), 'expert_bias': jnp.zeros((E,), jnp.float32), 'Wg': w(ks[6], (E, C, I)), 'Wu': w(ks[7], (E, C, I)), 'Wd': w(ks[8], (E, I, C)), 'sWg': w(ks[9], (S, C, I)), 'sWu': w(ks[10], (S, C, I)), 'sWd': w(ks[11], (S, I, C))}
    _L0_ffn_all = _L0_ffn_setup()
    _L0_ffn_in = {k: v for k, v in _L0_ffn_all.items() if k in ('w_ln1', 'Wq', 'Wkva', 'Wkvb', 'Wo', 'w_ln2', 'Wgate', 'expert_bias', 'Wg', 'Wu', 'Wd', 'sWg', 'sWu', 'sWd')}
    del _L0_ffn_all
    return {'x': x, 'ctx_1024': ctx_1024, 'g_xattn': g_xattn, 'g_ffn': g_ffn, 'L0_xattn_q_w': _L0_xattn_in['q_w'], 'L0_xattn_k_w': _L0_xattn_in['k_w'], 'L0_xattn_norm_w': _L0_xattn_in['norm_w'], 'L0_xattn_gate_w': _L0_xattn_in['gate_w'], 'L0_xattn_gate_b': _L0_xattn_in['gate_b'], 'L0_ffn_w_ln1': _L0_ffn_in['w_ln1'], 'L0_ffn_Wq': _L0_ffn_in['Wq'], 'L0_ffn_Wkva': _L0_ffn_in['Wkva'], 'L0_ffn_Wkvb': _L0_ffn_in['Wkvb'], 'L0_ffn_Wo': _L0_ffn_in['Wo'], 'L0_ffn_w_ln2': _L0_ffn_in['w_ln2'], 'L0_ffn_Wgate': _L0_ffn_in['Wgate'], 'L0_ffn_expert_bias': _L0_ffn_in['expert_bias'], 'L0_ffn_Wg': _L0_ffn_in['Wg'], 'L0_ffn_Wu': _L0_ffn_in['Wu'], 'L0_ffn_Wd': _L0_ffn_in['Wd'], 'L0_ffn_sWg': _L0_ffn_in['sWg'], 'L0_ffn_sWu': _L0_ffn_in['sWu'], 'L0_ffn_sWd': _L0_ffn_in['sWd']}

def reference(x, ctx_1024, g_xattn, g_ffn, L0_xattn_q_w, L0_xattn_k_w, L0_xattn_norm_w, L0_xattn_gate_w, L0_xattn_gate_b, L0_ffn_w_ln1, L0_ffn_Wq, L0_ffn_Wkva, L0_ffn_Wkvb, L0_ffn_Wo, L0_ffn_w_ln2, L0_ffn_Wgate, L0_ffn_expert_bias, L0_ffn_Wg, L0_ffn_Wu, L0_ffn_Wd, L0_ffn_sWg, L0_ffn_sWu, L0_ffn_sWd):
    import jax
    import jax.numpy as jnp

    def _L0_xattn_ref(hidden_states, memory_state, q_w, k_w, norm_w, gate_w, gate_b):
        import jax, jax.numpy as jnp
        import numpy as np
        EPS = 1e-06

        def _rmsnorm(x, w, eps=EPS):
            x32 = x.astype(jnp.float32)
            var = jnp.mean(x32 * x32, axis=-1, keepdims=True)
            return (x32 * jax.lax.rsqrt(var + eps)).astype(x.dtype) * w
        B, S, H = hidden_states.shape
        K = memory_state.shape[1]
        scale = 1.0 / np.sqrt(H)
        normed = _rmsnorm(hidden_states, norm_w)
        v_pool = jnp.concatenate([normed, memory_state], axis=1)
        q = jnp.einsum('bsh,oh->bso', normed, q_w)
        k = jnp.einsum('bth,oh->bto', v_pool, k_w)
        logits = jnp.einsum('bsd,btd->bst', q, k) * scale
        local = jnp.tril(jnp.ones((S, S), bool))
        mask = jnp.concatenate([local, jnp.ones((S, K), bool)], axis=1)
        logits = jnp.where(mask[None], logits, -jnp.inf)
        attn = jax.nn.softmax(logits, axis=-1)
        h_tilde = jnp.einsum('bst,bth->bsh', attn, v_pool)
        alpha = jax.nn.sigmoid(jnp.einsum('bsh,oh->bso', hidden_states, gate_w) + gate_b)
        return (1.0 - alpha) * hidden_states + alpha * h_tilde

    def _L0_ffn_ref(x, w_ln1, Wq, Wkva, Wkvb, Wo, w_ln2, Wgate, expert_bias, Wg, Wu, Wd, sWg, sWu, sWd):
        import jax, jax.numpy as jnp
        import numpy as np
        B, T, C = (2, 256, 128)
        H, D = (16, 64)
        CR = 8
        R = C // CR
        ROPE = D // 2
        NOPE = D - ROPE
        E, K, I, S = (8, 2, 64, 1)
        THETA = 100000.0
        EPS = 1e-05

        def _rmsnorm(x, w):
            rms = jnp.sqrt(jnp.mean(x * x, axis=-1, keepdims=True) + EPS)
            return w * (x / rms)

        def _rope(xh):
            d = xh.shape[-1]
            t = jnp.arange(xh.shape[2], dtype=jnp.float32)
            freqs = 1.0 / THETA ** (jnp.arange(0, d, 2, dtype=jnp.float32) / d)
            ang = jnp.outer(t, freqs)
            cos, sin = (jnp.cos(ang), jnp.sin(ang))
            xr = xh.reshape(xh.shape[:-1] + (d // 2, 2))
            x0, x1 = (xr[..., 0], xr[..., 1])
            rot = jnp.stack([x0 * cos - x1 * sin, x0 * sin + x1 * cos], axis=-1)
            return rot.reshape(xh.shape)

        def _attention(x, Wq, Wkva, Wkvb, Wo):
            b, t, _ = x.shape
            q = (x @ Wq).reshape(b, t, H, D).transpose(0, 2, 1, 3)
            ckv = x @ Wkva
            kv_latent, k_rope = (ckv[:, :, :R], ckv[:, :, R:])
            kv = (kv_latent @ Wkvb).reshape(b, t, H, NOPE).transpose(0, 2, 1, 3)
            k_rope = jnp.broadcast_to(k_rope[:, None, :, :], (b, H, t, ROPE))
            q_nope, q_rope = (q[..., :NOPE], q[..., NOPE:])
            q = jnp.concatenate([q_nope, _rope(q_rope)], axis=-1)
            k = jnp.concatenate([kv, _rope(k_rope)], axis=-1)
            v = jnp.concatenate([kv, jnp.zeros_like(k_rope)], axis=-1)
            att = jnp.einsum('bhqd,bhkd->bhqk', q, k) / jnp.sqrt(jnp.float32(D))
            mask = jnp.tril(jnp.ones((t, t), dtype=bool))
            att = jnp.where(mask, att, jnp.float32(-jnp.inf))
            att = jax.nn.softmax(att, axis=-1)
            y = jnp.einsum('bhqk,bhkd->bhqd', att, v)
            y = y.transpose(0, 2, 1, 3).reshape(b, t, H * D)
            return y @ Wo

        def _experts(x_flat, Wg, Wu, Wd):
            g = jax.nn.silu(jnp.einsum('nc,eci->nei', x_flat, Wg))
            u = jnp.einsum('nc,eci->nei', x_flat, Wu)
            return jnp.einsum('nei,eic->nec', g * u, Wd)

        def _moe(x, Wgate, expert_bias, Wg, Wu, Wd, sWg, sWu, sWd):
            b, t, c = x.shape
            xf = x.reshape(-1, c)
            shared = jnp.mean(_experts(xf, sWg, sWu, sWd), axis=1)
            logits = xf @ Wgate + expert_bias
            probs = jax.nn.softmax(logits, axis=-1)
            topk_p, topk_i = jax.lax.top_k(probs, K)
            topk_p = topk_p / jnp.sum(topk_p, axis=-1, keepdims=True)
            comb = jnp.sum(jax.nn.one_hot(topk_i, E, dtype=xf.dtype) * topk_p[..., None], axis=1)
            routed = jnp.einsum('ne,nec->nc', comb, _experts(xf, Wg, Wu, Wd))
            return (shared + routed).reshape(b, t, c)
        x = x + _attention(_rmsnorm(x, w_ln1), Wq, Wkva, Wkvb, Wo)
        residual = x
        xn = _rmsnorm(x, w_ln2)
        x_out = _moe(xn, Wgate, expert_bias, Wg, Wu, Wd, sWg, sWu, sWd)
        return residual + x_out
    x = x + jnp.tanh(g_xattn[0]) * _L0_xattn_ref(_layernorm(x, axis=-1), ctx_1024, L0_xattn_q_w, L0_xattn_k_w, L0_xattn_norm_w, L0_xattn_gate_w, L0_xattn_gate_b)
    x = x + jnp.tanh(g_ffn[0]) * _L0_ffn_ref(_layernorm(x, axis=-1), L0_ffn_w_ln1, L0_ffn_Wq, L0_ffn_Wkva, L0_ffn_Wkvb, L0_ffn_Wo, L0_ffn_w_ln2, L0_ffn_Wgate, L0_ffn_expert_bias, L0_ffn_Wg, L0_ffn_Wu, L0_ffn_Wd, L0_ffn_sWg, L0_ffn_sWu, L0_ffn_sWd)
    return x

_drawn_inputs = setup_inputs


def setup_inputs(seed=0):
    import zlib

    import numpy as np

    out = dict(_drawn_inputs(seed))
    spreads = {'L0_xattn_norm_w': (1.0, 0.6),
     'L0_xattn_gate_b': (0.0, 0.527),
     'L0_ffn_w_ln1': (1.0, 0.6),
     'L0_ffn_w_ln2': (1.0, 0.6),
     'L0_ffn_expert_bias': (0.0, 0.8)}
    factors = {'L0_ffn_Wq': 8.0,
     'L0_ffn_Wkva': 8.0,
     'L0_ffn_Wkvb': 8.0,
     'L0_ffn_Wo': 8.0,
     'L0_ffn_Wgate': 8.0,
     'L0_ffn_Wg': 8.0,
     'L0_ffn_Wu': 8.0,
     'L0_ffn_Wd': 8.0,
     'L0_ffn_sWg': 5.618,
     'L0_ffn_sWu': 5.521,
     'L0_ffn_sWd': 5.641}
    for name, (base, spread) in spreads.items():
        noise = np.random.default_rng([zlib.crc32(name.encode()), seed]).standard_normal(out[name].shape)
        drawn = base * np.exp(spread * noise) if base else spread * noise
        out[name] = jnp.asarray(drawn.astype(out[name].dtype))
    for name, factor in factors.items():
        out[name] = (out[name] * factor).astype(out[name].dtype)
    return out
```

```python
import numpy as np
import concourse.bass as bass
from concourse import mybir
from contextlib import ExitStack

B, S, C = 8, 256, 128
P = 128
NT = S // P
NH, DH, NOPE, ROPE = 16, 64, 32, 32
HALF = ROPE // 2
R = 16
KD = R + ROPE
NI = 4
NE, EI = 8, 64
NP = NE // 2
QROW = 2 * KD
NEG = -1.0e30


def build(nc, t_in, out_d):
    f32, f32r, bf16 = mybir.dt.float32, mybir.dt.float32r, mybir.dt.bfloat16
    ACT, ALU, AX = mybir.ActivationFunctionType, mybir.AluOpType, mybir.AxisListType
    ctx = ExitStack()
    with ctx:
        def sb(name, shape, dt=f32):
            return ctx.enter_context(nc.sbuf_tensor(name, shape, dt))

        def pb(name):
            return ctx.enter_context(nc.psum_tensor(name, [P, 512], f32))

        def sem(name):
            return ctx.enter_context(nc.semaphore(name))

        ident = sb("ident", [P, P])
        mask_f = sb("mask_f", [P, P])
        rope_cs = sb("rope_cs", [P, NT, 3, HALF])
        sel = sb("sel", [NE, NP, P])
        rank = sb("rank", [P, NE])
        ones_row = sb("ones_row", [1, P])
        wq_raw = sb("wq_raw", [P, NH, DH])
        wkva_raw = sb("wkva_raw", [P, KD])
        wkvb_raw = sb("wkvb_raw", [R, NI, NI, NOPE])
        wo_g = sb("wo_g", [P, NI, C])
        xq_w = sb("xq_w", [P, C])
        xk_w = sb("xk_w", [P, C])
        xg_w = sb("xg_w", [P, C])
        gate_b = sb("gate_b", [1, C])
        normw_b = sb("normw_b", [P, C])
        ln1_w = sb("ln1_w", [P, 1])
        ln2_w = sb("ln2_w", [P, 1])
        gx = sb("gx", [P, 1])
        gf = sb("gf", [P, 1])
        ebias = sb("ebias", [1, NE])
        wgate_raw = sb("wgate_raw", [P, NE])
        wg_raw = sb("wg_raw", [P, NE + 1, EI])
        wu_raw = sb("wu_raw", [P, NE + 1, EI])
        wd = sb("wd", [P, NP, C])
        swd = sb("swd", [EI, C])

        identb = sb("identb", [P, P], bf16)
        maskb = sb("maskb", [P, P], bf16)
        ln1_s = sb("ln1_s", [P, 1])
        tgx = sb("tgx", [P, 1])
        tgf = sb("tgf", [P, 1])
        wqn = sb("wqn", [P, NI, NI, NOPE])
        wqnT = sb("wqnT", [P, NI, P])
        bd = sb("bd", [P, NI, P])
        wn = sb("wn", [P, NH, R])
        wr = sb("wr", [P, NH, 2, HALF])
        ka = sb("ka", [P, KD])
        wvo = sb("wvo", [P, NI, C])
        aqk = sb("aqk", [P, C])
        xgT = sb("xgT", [P, C])
        wgate = sb("wgate", [P, NE])
        wg = sb("wg", [P, NE + 1, EI])
        wu = sb("wu", [P, NE + 1, EI])

        x_all = sb("x_all", [P, B * NT, C])
        c_all = sb("c_all", [P, B * NT, C])
        xi = sb("xi", [P, NT, C])
        cx = sb("cx", [P, NT, C])
        h2 = sb("h2", [P, NT, C])

        st = sb("st", [P, NT, 6])
        mv = sb("mv", [P, NT, 2])
        nhalf = sb("nhalf", [P, 2, NT])
        vv = sb("vv", [P, 2, NT])
        ss = sb("ss", [P, 2, NT])
        tmp2 = sb("tmp2", [P, NT])
        hx = sb("hx", [P, NT, C])
        vx = sb("vx", [P, NT, C])
        poolT = sb("poolT", [P, 2 * S])
        hT = sb("hT", [P, S])
        qxT = sb("qxT", [P, S])
        nmx = sb("nmx", [P, NT])
        rsx = sb("rsx", [P, NT])
        px = sb("px", [P, NT, 2 * S])
        pxT = sb("pxT", [P, 7, P])
        dx = sb("dx", [P, NT, C])
        thx = sb("thx", [P, NT, C])
        st2 = sb("st2", [P, NT, 6])
        mv2 = sb("mv2", [P, NT, 2])
        vv2 = sb("vv2", [P, 2, NT])
        ss2 = sb("ss2", [P, 2, NT])
        xn = sb("xn", [P, NT, C])
        xnT = sb("xnT", [P, S])

        lat1 = sb("lat1", [P, NT, 2 * R])
        kf = sb("kf", [P, NT, KD])
        kt1 = sb("kt1", [P, NT, 2, HALF])
        kt2 = sb("kt2", [P, NT, 2, HALF])
        ks = sb("ks", [P, 2, NT, P], f32r)
        kT = sb("kT", [P, 2, NT, P], f32r)
        q1 = sb("q1", [P, NH, 2, HALF])
        q2 = sb("q2", [P, NH, 2, HALF])
        qf = sb("qf", [P, NH, KD])
        qs = sb("qs", [P, NH, 2, KD], f32r)
        qT = sb("qT", [P, NT, NH, P], f32r)
        mx = sb("mx", [P, NT, NH])
        mT = sb("mT", [NH, NT, P], f32r)
        pT = sb("pT", [P, 2, NI, 512])
        den = sb("den", [P, 512])
        rden = sb("rden", [P, 512])
        ya = sb("ya", [P, 512])

        sq = sb("sq", [P, NT, C])
        ms = sb("ms", [P, NT])
        r3 = sb("r3", [P, NT])
        xn3 = sb("xn3", [P, NT, C])
        n3T = sb("n3T", [P, S])
        lg = sb("lg", [P, NT, NE])
        m1 = sb("m1", [P, NT, 1])
        m2 = sb("m2", [P, NT, 1])
        ra = sb("ra", [P, NT, NE])
        ra1 = sb("ra1", [P, NT, 1])
        rb1 = sb("rb1", [P, NT, 1])
        oh1 = sb("oh1", [P, NT, NE])
        oh2 = sb("oh2", [P, NT, NE])
        l2 = sb("l2", [P, NT, NE])
        dm = sb("dm", [P, NT, 1])
        e2 = sb("e2", [P, NT, 1])
        p1 = sb("p1", [P, NT, 1])
        p2 = sb("p2", [P, NT, 1])
        comb = sb("comb", [P, NT, NE])
        combT = sb("combT", [NE, S])
        th = sb("th", [P, NP + 1, S])
        s1 = sb("s1", [P, NP + 1, S])
        hid = sb("hid", [P, NP + 1, S])
        fin = sb("fin", [P, NT, C])
        outt = sb("outt", [P, NT, C])

        pA = [pb("pA0"), pb("pA1")]
        pB = [pb("pB0"), pb("pB1")]
        pV = pb("pV")
        w0, w1, w2 = pb("w0"), pb("w1"), pb("w2")

        names = """consts_in weights_in xw_in x_in consts_ready wqn_ready wqnT_psum wqnT_ready wkvbT_psum
            bd_ready absorb_psum setup_psum2 aqk_ready wn_ready weights_ready act_setup pool_setup
            front_norm frontT_psum frontT_act frontT_dve qx_psum qx_ready lx_psum nmx_ready px_ready
            pxT_psum pxT_act pxT_dve hx_psum thx_ready xn_ready xnT_psum xnT_ready
            ckv_psum k_lat k_split ksT_psum kT_ready q_psum q_rope12 q_nope q_full q_high q_low qT_psum qT_ready
            a_psum mx_ready mT_psum mT_ready minus_max_in b_psum exp_ready masked pv_psum ya_ready y_psum
            x3_ready xn3_ready n3T_psum n3T_ready lg_psum dm_ready e2_ready comb_ready combT_psum combT_ready
            combB_psum gu_psum th_ready hid_ready moe_psum out_ready out_done
            dve_chain dve_passed pool_passed var1_ready var2_ready var3_ready scale1_ready scale2_ready scale3_ready""".split()
        s = {n: sem(n) for n in names}

        class Chain:

            def __init__(self, eng, sem_, per=0, i=0, base=0):
                self.eng, self.sem, self.at, self.n = eng, sem_, base + per * i, 0

            def __call__(self, ins):
                self.n += 1
                ins.then_inc(self.sem, 1)
                self.eng.wait_ge(self.sem, self.at + self.n)

        DVE_SETUP, DVE_PER = 2, 57
        block = ctx.enter_context(nc.Block())

        @block.sync
        def _(sp):
            n = 0
            for dst, src in [(ident[:], t_in["c_ident"]), (mask_f[:], t_in["c_mask"]), (rope_cs[:], t_in["c_rope"]),
                             (sel[:], t_in["c_sel"]), (rank[:], t_in["c_rank"]), (ones_row[:], t_in["c_ones"])]:
                sp.dma_start(dst, src).then_inc(s["consts_in"], 16)
            sp.dma_start(ln1_w[:], t_in["L0_ffn_w_ln1"].rearrange("(c a) -> c a", a=1)).then_inc(s["weights_in"], 16)
            sp.dma_start(ln2_w[:], t_in["L0_ffn_w_ln2"].rearrange("(c a) -> c a", a=1)).then_inc(s["weights_in"], 16)
            sp.dma_start(wq_raw[:], t_in["L0_ffn_Wq"].rearrange("c (h d) -> c h d", h=NH)).then_inc(s["weights_in"], 16)
            wkvb_v = t_in["L0_ffn_Wkvb"].rearrange("l (j i d) -> i l j d", j=NI, i=NI)
            for m in range(NI):
                sp.dma_start(wkvb_raw[:, m, :, :], wkvb_v[m]).then_inc(s["weights_in"], 16)
            sp.dma_start(wkva_raw[:], t_in["L0_ffn_Wkva"]).then_inc(s["weights_in"], 16)
            wo_v = t_in["L0_ffn_Wo"].rearrange("(j i e d) c -> j e d i c", j=NI, i=NI, e=2)
            for j in range(NI):
                sp.dma_start(wo_g[NOPE * j:NOPE * (j + 1), :, :], wo_v[j, 0]).then_inc(s["weights_in"], 16)
            sp.dma_start(wgate_raw[:], t_in["L0_ffn_Wgate"]).then_inc(s["weights_in"], 16)
            sp.dma_start(ebias[:], t_in["L0_ffn_expert_bias"].rearrange("(a e) -> a e", a=1)).then_inc(s["weights_in"], 16)
            for dst, big, small in [(wg_raw, "L0_ffn_Wg", "L0_ffn_sWg"), (wu_raw, "L0_ffn_Wu", "L0_ffn_sWu")]:
                sp.dma_start(dst[:, 0:NE, :], t_in[big].rearrange("e c i -> c e i")).then_inc(s["weights_in"], 16)
                sp.dma_start(dst[:, NE, :], t_in[small][0]).then_inc(s["weights_in"], 16)
            sp.dma_start(wd[:], t_in["L0_ffn_Wd"].rearrange("(p e) i c -> (e i) p c", e=2)).then_inc(s["weights_in"], 16)
            sp.dma_start(swd[:], t_in["L0_ffn_sWd"][0]).then_inc(s["weights_in"], 16)

            sp.dma_start(x_all[:], t_in["x"].rearrange("b (t p) c -> p (b t) c", p=P)).then_inc(s["x_in"], 16)
            sp.dma_start(c_all[:], t_in["ctx_1024"].rearrange("b (t p) c -> p (b t) c", p=P)).then_inc(s["x_in"], 16)
            with sp.Fori(0, B) as i:
                for t in range(NT):
                    sp.wait_ge(s["mT_ready"], NT * i + t + 1)
                    sp.dma_start(qT[QROW:QROW + 1, t, :, :].bitcast(f32), mT[:, t, :].bitcast(f32)).then_inc(s["minus_max_in"], 16)
                sp.wait_ge(s["out_ready"], i + 1)
                sp.dma_start(out_d[bass.ds(i, 1), :, :].rearrange("b (t p) c -> p (b t) c", p=P), outt[:]).then_inc(s["out_done"], 16)
            sp.wait_ge(s["out_done"], 16 * B)

        NW = 16 * 20

        @block.gpsimd
        def _(pool):
            for dst, src in [(xq_w[:], t_in["L0_xattn_q_w"]), (xk_w[:], t_in["L0_xattn_k_w"]), (xg_w[:], t_in["L0_xattn_gate_w"]),
                             (gate_b[:], t_in["L0_xattn_gate_b"].rearrange("(a c) -> a c", a=1)),
                             (normw_b[:], t_in["L0_xattn_norm_w"].partition_broadcast(P)),
                             (gx[:], t_in["g_xattn"].partition_broadcast(P)), (gf[:], t_in["g_ffn"].partition_broadcast(P))]:
                pool.dma_start(dst, src).then_inc(s["xw_in"], 16)
            pool.memset(bd[:], 0.0).then_inc(s["pool_setup"], 1)
            pool.memset(lat1[:], 1.0).then_inc(s["pool_setup"], 1)
            pool.memset(nhalf[:], -0.5).then_inc(s["pool_setup"], 1)
            pool.wait_ge(s["pool_setup"], 3)
            with pool.Fori(0, B) as i:
                pool.wait_ge(s["var1_ready"], i + 1)
                pool.tensor_tensor(ss[:], vv[:], nhalf[:], ALU.pow).then_inc(s["scale1_ready"], 1)
                pool.wait_ge(s["var2_ready"], i + 1)
                pool.tensor_tensor(ss2[:], vv2[:], nhalf[:], ALU.pow).then_inc(s["scale2_ready"], 1)
                for t in range(NT):
                    pool.wait_ge(s["q_rope12"], NT * i + t + 1)
                    pool.tensor_tensor(qf[:, :, R:KD], q1[:].rearrange("p h e d -> p h (e d)"),
                                       q2[:].rearrange("p h e d -> p h (e d)"), ALU.add).then_inc(s["q_full"], 1)
                    pool.wait_ge(s["q_high"], NT * i + t + 1)
                    pool.tensor_tensor(qs[:, :, 1, :], qf[:], qs[:, :, 0, :].bitcast(f32), ALU.subtract).then_inc(s["q_low"], 1)
                for t in range(NT):
                    for g in range(NI):
                        pool.wait_ge(s["exp_ready"], 12 * i + (0 if t == 0 else 4) + (g + 1 if t == 0 else 4 + g + 1))
                        pool.sem_inc(s["pool_passed"], 1)
                        pool.affine_select(out=pT[:, t, g, :], in_=pT[:, t, g, :], compare_op=ALU.is_ge, fill=0.0,
                                           base=0, pattern=[[0, NI], [1, P]], channel_multiplier=-1).then_inc(s["masked"], 1)
                pool.wait_ge(s["var3_ready"], i + 1)
                pool.tensor_tensor(r3[:], ms[:], nhalf[:, 0, :], ALU.pow).then_inc(s["scale3_ready"], 1)

        @block.scalar
        def _(act):
            act.wait_ge(s["xw_in"], 16 * 7)
            act.activation(tgx[:], gx[:], ACT.Tanh).then_inc(s["act_setup"], 1)
            act.activation(tgf[:], gf[:], ACT.Tanh).then_inc(s["act_setup"], 1)
            act.wait_ge(s["weights_in"], NW)
            act.activation(ln1_s[:], ln1_w[:], ACT.Copy, scale=DH ** -0.5).then_inc(s["act_setup"], 1)
            act.wait_ge(s["act_setup"], 3)
            act.activation(wqn[:], wq_raw[:, :, 0:NOPE].rearrange("p (j i) d -> p i j d", i=NI), ACT.Copy, scale=ln1_s[:, 0:1]).then_inc(s["wqn_ready"], 1)
            act.activation(wr[:].rearrange("p h e d -> p h d e"), wq_raw[:, :, NOPE:DH].rearrange("p h (d e) -> p h d e", e=2), ACT.Copy, scale=ln1_s[:, 0:1]).then_inc(s["act_setup"], 1)
            act.activation(ka[:, 0:R], wkva_raw[:, 0:R], ACT.Copy, scale=ln1_w[:, 0:1]).then_inc(s["act_setup"], 1)
            act.activation(ka[:, R:KD].rearrange("p (e d) -> p d e", e=2), wkva_raw[:, R:KD].rearrange("p (d e) -> p d e", e=2), ACT.Copy, scale=ln1_w[:, 0:1]).then_inc(s["act_setup"], 1)
            act.activation(wgate[:], wgate_raw[:], ACT.Copy, scale=ln2_w[:, 0:1]).then_inc(s["act_setup"], 1)
            act.activation(wg[:], wg_raw[:], ACT.Copy, scale=ln2_w[:, 0:1]).then_inc(s["act_setup"], 1)
            act.activation(wu[:], wu_raw[:], ACT.Copy, scale=ln2_w[:, 0:1]).then_inc(s["act_setup"], 1)
            act.wait_ge(s["setup_psum2"], 1)
            act.activation(aqk[:], pV[:, 0:C], ACT.Copy, scale=C ** -0.5).then_inc(s["act_setup"], 1)
            act.activation(xgT[:], pV[:, C:2 * C], ACT.Copy).then_inc(s["act_setup"], 1)
            act.wait_ge(s["wqnT_psum"], 1)
            act.activation(wqnT[:], w0[:].rearrange("p (i c) -> p i c", i=NI), ACT.Copy).then_inc(s["wqnT_ready"], 1)
            act.wait_ge(s["absorb_psum"], 1)
            act.activation(wn[:].rearrange("p (j i) l -> p i j l", i=NI),
                           w1[:].rearrange("p (i j l) -> p i j l", i=NI, j=NI)[:, :, :, 0:R], ACT.Copy).then_inc(s["act_setup"], 1)
            act.activation(wvo[:], w2[:].rearrange("p (i c) -> p i c", i=NI), ACT.Copy).then_inc(s["weights_ready"], 1)

            with act.Fori(0, B) as i:
                act.wait_ge(s["frontT_psum"], i + 1)
                act.activation(poolT[:], w0[:], ACT.Copy).then_inc(s["frontT_act"], 1)
                act.wait_ge(s["qx_psum"], i + 1)
                act.activation(qxT[:], w2[:, 0:S], ACT.Copy).then_inc(s["qx_ready"], 1)
                for t in range(NT):
                    act.wait_ge(s["nmx_ready"], NT * i + t + 1)
                    n = P * (t + 1) + S
                    act.activation(px[:, t, 0:n], [w0, w1][t][:, 0:n], ACT.Exp, bias=nmx[:, t:t + 1], accum_out=rsx[:, t:t + 1]).then_inc(s["px_ready"], 1)
                act.wait_ge(s["pxT_psum"], i + 1)
                act.activation(pxT[:, 0:4, :], w2[:].rearrange("p (k q) -> p k q", k=4), ACT.Copy).then_inc(s["pxT_act"], 1)
                act.wait_ge(s["hx_psum"], i + 1)
                act.activation(thx[:], w1[:, S:2 * S].rearrange("p (t c) -> p t c", t=NT), ACT.Tanh, scale=0.5).then_inc(s["thx_ready"], 1)
                act.wait_ge(s["xnT_psum"], i + 1)
                act.activation(xnT[:], w2[:, 0:S], ACT.Copy).then_inc(s["xnT_ready"], 1)
                act.wait_ge(s["ckv_psum"], i + 1)
                ckv = w0[:, 0:NT * KD].rearrange("p (t d) -> p t d", t=NT)
                act.activation(lat1[:, :, 0:R], ckv[:, :, 0:R], ACT.Copy).then_inc(s["k_lat"], 1)
                act.activation(kf[:, :, 0:R], ckv[:, :, 0:R], ACT.Copy).then_inc(s["k_lat"], 1)
                act.wait_ge(s["ksT_psum"], i + 1)
                act.activation(kT[:], w1[:].rearrange("p (e t q) -> p e t q", e=2, t=NT), ACT.Copy).then_inc(s["kT_ready"], 1)
                for t in range(NT):
                    act.wait_ge(s["q_psum"], NT * i + t + 1)
                    act.activation(qf[:, :, 0:R], w1[:, 0:NH * R].rearrange("p (h l) -> p h l", h=NH), ACT.Copy).then_inc(s["q_nope"], 1)
                    act.wait_ge(s["q_full"], NT * i + t + 1)
                    act.wait_ge(s["q_nope"], NT * i + t + 1)
                    act.activation(qs[:, :, 0, :], qf[:], ACT.Copy).then_inc(s["q_high"], 1)
                    for g in range(NI):
                        act.wait_ge(s["qT_psum"], 8 * i + 4 * t + g + 1)
                        act.activation(qT[0:QROW, t, NI * g:NI * (g + 1), :], [w0, w1][g % 2][0:QROW, :].rearrange("p (h q) -> p h q", h=NI), ACT.Copy).then_inc(s["qT_ready"], 1)
                n = 0
                for t in range(NT):
                    act.wait_ge(s["mT_psum"], NT * i + t + 1)
                    act.activation(mT[:, t, :], w2[0:NH, 0:P], ACT.Copy, scale=-1.0).then_inc(s["mT_ready"], 1)
                    for kt in range(t + 1):
                        for g in range(NI):
                            n += 1
                            act.wait_ge(s["b_psum"], 12 * i + n)
                            act.activation(pT[:, kt, g, :], pB[n % 2][:], ACT.Exp).then_inc(s["exp_ready"], 1)
                act.wait_ge(s["n3T_psum"], i + 1)
                act.activation(n3T[:], w0[:, 0:S], ACT.Copy).then_inc(s["n3T_ready"], 1)
                act.wait_ge(s["dm_ready"], i + 1)
                act.activation(e2[:], dm[:], ACT.Exp).then_inc(s["e2_ready"], 1)
                act.wait_ge(s["combT_psum"], i + 1)
                act.activation(combT[:], w2[0:NE, 0:S], ACT.Copy).then_inc(s["combT_ready"], 1)
                for p in range(NP + 1):
                    rows = P if p < NP else EI
                    act.wait_ge(s["gu_psum"], (NP + 1) * i + p + 1)
                    act.activation(th[0:rows, p, :], pA[p % 2][0:rows, 0:S], ACT.Tanh, scale=0.5).then_inc(s["th_ready"], 1)

        @block.tensor
        def _(pe):
            def mm(out, lhsT, rhs, start=True, stop=True):
                return pe.matmul(out, lhsT, rhs, start=start, stop=stop)

            pe.wait_ge(s["consts_in"], 16 * 6)
            pe.wait_ge(s["xw_in"], 16 * 7)
            mm(pV[:, 0:C], xq_w[:], xk_w[:])
            pe.transpose(pV[:, C:2 * C], xg_w[:], ident[:]).then_inc(s["setup_psum2"], 1)
            pe.wait_ge(s["weights_in"], NW)
            for m in range(NI):
                last = pe.transpose(w1[:, R * m:R * (m + 1)], wkvb_raw[:, m, :, :].rearrange("l j d -> l (j d)"), ident[0:R, 0:R])
            last.then_inc(s["wkvbT_psum"], 1)
            pe.wait_ge(s["wqn_ready"], 1)
            for m in range(NI):
                last = pe.transpose(w0[:, P * m:P * (m + 1)], wqn[:, m, :, :].rearrange("p j d -> p (j d)"), ident[:])
            last.then_inc(s["wqnT_psum"], 1)
            pe.wait_ge(s["bd_ready"], 1)
            pe.wait_ge(s["wqnT_ready"], 1)
            for m in range(NI):
                mm(w1[:, P * m:P * (m + 1)], wqnT[:, m, :], bd[:, m, :])
                last = mm(w2[:, P * m:P * (m + 1)], bd[:, m, :], wo_g[:, m, :])
            last.then_inc(s["absorb_psum"], 1)
            pe.wait_ge(s["weights_ready"], 1)
            pe.wait_ge(s["consts_ready"], 1)

            with pe.Fori(0, B) as i:
                pe.wait_ge(s["front_norm"], i + 1)
                for t in range(NT):
                    pe.transpose(w0[:, P * t:P * (t + 1)], vx[:, t, :], ident[:])
                    pe.transpose(w0[:, S + P * t:S + P * (t + 1)], cx[:, t, :], ident[:])
                for t in range(NT):
                    last = pe.transpose(w1[:, P * t:P * (t + 1)], hx[:, t, :], ident[:])
                last.then_inc(s["frontT_psum"], 1)
                pe.wait_ge(s["frontT_act"], i + 1)
                mm(w2[:, 0:S], aqk[:], poolT[:, 0:S]).then_inc(s["qx_psum"], 1)
                pe.wait_ge(s["qx_ready"], i + 1)
                pe.wait_ge(s["frontT_dve"], i + 1)
                for t in range(NT):
                    w = [w0, w1][t]
                    q = qxT[:, P * t:P * (t + 1)]
                    if t == 0:
                        mm(w[:, 0:P], q, poolT[:, 0:P], stop=False)
                        mm(w[:, 0:P], identb[:], maskb[:], start=False)
                        mm(w[:, P:P + S], q, poolT[:, S:2 * S]).then_inc(s["lx_psum"], 1)
                    else:
                        mm(w[:, 0:2 * S], q, poolT[:], stop=False)
                        mm(w[:, P:2 * P], identb[:], maskb[:], start=False).then_inc(s["lx_psum"], 1)
                pe.wait_ge(s["px_ready"], NT * i + NT)
                for k in range(4):
                    pe.transpose(w2[:, P * k:P * (k + 1)], px[:, 1, P * k:P * (k + 1)], ident[:])
                for k in range(3):
                    last = pe.transpose(w0[:, P * k:P * (k + 1)], px[:, 0, P * k:P * (k + 1)], ident[:])
                last.then_inc(s["pxT_psum"], 1)
                for t in range(NT):
                    mm(w1[:, S + P * t:S + P * (t + 1)], hT[:, P * t:P * (t + 1)], xgT[:], stop=False)
                    mm(w1[:, S + P * t:S + P * (t + 1)], ones_row[:], gate_b[:], start=False)
                pe.wait_ge(s["pxT_act"], i + 1)
                pe.wait_ge(s["pxT_dve"], i + 1)
                vals = [vx[:, 0, :], vx[:, 1, :], cx[:, 0, :], cx[:, 1, :]]
                for k, v in enumerate([vals[0], vals[2], vals[3]]):
                    mm(w2[:, 0:P], pxT[:, 4 + k, :], v, start=k == 0, stop=k == 2)
                for k, v in enumerate(vals):
                    last = mm(w2[:, P:2 * P], pxT[:, k, :], v, start=k == 0, stop=k == 3)
                last.then_inc(s["hx_psum"], 1)
                pe.wait_ge(s["xn_ready"], i + 1)
                for t in range(NT):
                    last = pe.transpose(w2[:, P * t:P * (t + 1)], xn[:, t, :], ident[:])
                last.then_inc(s["xnT_psum"], 1)
                pe.wait_ge(s["xnT_ready"], i + 1)
                for t in range(NT):
                    last = mm(w0[:, KD * t:KD * (t + 1)], xnT[:, P * t:P * (t + 1)], ka[:])
                last.then_inc(s["ckv_psum"], 1)
                pe.wait_ge(s["k_split"], i + 1)
                for e in range(2):
                    for t in range(NT):
                        last = pe.transpose(w1[:, (NT * e + t) * P:(NT * e + t + 1) * P], ks[:, e, t, :].bitcast(f32), ident[:])
                last.then_inc(s["ksT_psum"], 1)
                for t in range(NT):
                    if t == 0:
                        pe.wait_ge(s["kT_ready"], i + 1)
                    else:
                        pe.wait_ge(s["qT_ready"], 8 * i + 4)
                    q = xnT[:, P * t:P * (t + 1)]
                    mm(w0[:], q, wr[:].rearrange("p h e d -> p (h e d)"))
                    mm(w1[:, 0:NH * R], q, wn[:].rearrange("p h l -> p (h l)")).then_inc(s["q_psum"], 1)
                    pe.wait_ge(s["q_low"], NT * i + t + 1)
                    for g in range(NI):
                        if g >= 2:
                            pe.wait_ge(s["qT_ready"], 8 * i + 4 * t + g - 1)
                        for h in range(NI):
                            last = pe.transpose([w0, w1][g % 2][0:QROW, P * h:P * (h + 1)], qs[:, NI * g + h, :, :].bitcast(f32).rearrange("p e d -> p (e d)"), ident[:])
                        last.then_inc(s["qT_psum"], 1)
                n = 0
                for t in range(NT):
                    pe.wait_ge(s["qT_ready"], 8 * i + 4 * t + 4)
                    nk = P * (t + 1)
                    per = 512 // nk
                    for u in range(NH // per):
                        n += 1
                        if n > 2:
                            pe.wait_ge(s["mx_ready"], 12 * i + n - 2)
                        w = pA[n % 2]
                        for h in range(per):
                            mm(w[:, nk * h:nk * (h + 1)], qT[0:QROW, t, per * u + h, :],
                               kT[0:QROW, 0, 0:t + 1, :].rearrange("p t q -> p (t q)"), start=h == 0, stop=False)
                        mm(w[:].rearrange("p (h k) -> p h k", h=per)[:, :, P * t:P * (t + 1)], identb[:],
                           maskb[:].unsqueeze(1).to_broadcast([P, per, P]), start=False).then_inc(s["a_psum"], 1)
                    pe.wait_ge(s["mx_ready"], 12 * i + n)
                    if t == 1:
                        pe.wait_ge(s["mT_ready"], NT * i + 1)
                    pe.transpose(w2[0:NH, 0:P], mx[:, t, :], ident[:]).then_inc(s["mT_psum"], 1)
                n = 0
                for t in range(NT):
                    pe.wait_ge(s["minus_max_in"], 16 * NT * i + 16 * (t + 1))
                    for kt in range(t + 1):
                        for g in range(NI):
                            n += 1
                            if n > 2:
                                pe.wait_ge(s["exp_ready"], 12 * i + n - 2)
                            q = qT[0:QROW + 1, t, NI * g:NI * (g + 1), :].rearrange("p h q -> p (h q)")
                            mm(pB[n % 2][:], kT[0:QROW + 1, 0, kt, :], q, stop=False)
                            mm(pB[n % 2][:], kT[0:QROW + 1, 1, kt, :], q, start=False).then_inc(s["b_psum"], 1)
                    if t == 1:
                        pe.wait_ge(s["ya_ready"], NT * i + 1)
                    for kt in range(t + 1):
                        pe.wait_ge(s["masked"], 8 * i + 4 * t + 4) if kt == t else pe.wait_ge(s["exp_ready"], 12 * i + 8)
                        for g in range(NI):
                            last = mm(pV[32 * g:32 * (g + 1), :], lat1[:, kt, :], pT[:, kt, g, :], start=kt == 0, stop=kt == t)
                    last.then_inc(s["pv_psum"], 1)
                    pe.wait_ge(s["ya_ready"], NT * i + t + 1)
                    for m in range(NI):
                        last = mm(w1[:, P * t:P * (t + 1)], ya[:, P * m:P * (m + 1)], wvo[:, m, :], start=m == 0, stop=m == NI - 1)
                    last.then_inc(s["y_psum"], 1)
                pe.wait_ge(s["xn3_ready"], i + 1)
                for t in range(NT):
                    last = pe.transpose(w0[:, P * t:P * (t + 1)], xn3[:, t, :], ident[:])
                last.then_inc(s["n3T_psum"], 1)
                pe.wait_ge(s["n3T_ready"], i + 1)
                for t in range(NT):
                    mm(w2[:, NE * t:NE * (t + 1)], n3T[:, P * t:P * (t + 1)], wgate[:], stop=False)
                    last = mm(w2[:, NE * t:NE * (t + 1)], ones_row[:], ebias[:], start=False)
                last.then_inc(s["lg_psum"], 1)
                for p in range(NP + 1):
                    rows = P if p < NP else EI
                    if p == 1:
                        pe.wait_ge(s["comb_ready"], i + 1)
                        for t in range(NT):
                            last = pe.transpose(w2[0:NE, P * t:P * (t + 1)], comb[:, t, :], ident[:])
                        last.then_inc(s["combT_psum"], 1)
                        pe.wait_ge(s["combT_ready"], i + 1)
                        for q in range(NP):
                            last = mm(pB[q // 2][:, S * (q % 2):S * (q % 2 + 1)], sel[:, q, :], combT[:])
                        last.then_inc(s["combB_psum"], 1)
                    if p >= 2:
                        pe.wait_ge(s["hid_ready"], (NP + 1) * i + p - 1)
                    w = pA[p % 2]
                    last_e = min(2 * p + 2, NE + 1)
                    mm(w[0:rows, 0:S], wg[:, 2 * p:last_e, :].rearrange("p e i -> p (e i)"), n3T[:])
                    mm(w[0:rows, S:2 * S], wu[:, 2 * p:last_e, :].rearrange("p e i -> p (e i)"), n3T[:]).then_inc(s["gu_psum"], 1)
                pe.wait_ge(s["hid_ready"], (NP + 1) * (i + 1))
                for t in range(NT):
                    for p in range(NP):
                        mm(w0[:, P * t:P * (t + 1)], hid[:, p, P * t:P * (t + 1)], wd[:, p, :], start=p == 0, stop=False)
                    last = mm(w0[:, P * t:P * (t + 1)], hid[0:EI, NP, P * t:P * (t + 1)], swd[:], start=False)
                last.then_inc(s["moe_psum"], 1)

        @block.vector
        def _(dve):
            V = nc.vector
            dve.wait_ge(s["consts_in"], 16 * 6)
            V.tensor_copy(identb[:], ident[:])
            V.tensor_copy(maskb[:], mask_f[:])
            V.memset(ks[:].bitcast(f32), 0.0)
            link = Chain(dve, s["dve_chain"])
            link(V.memset(kf[:], 0.0))
            link(V.memset(ks[:, 0, :, QROW:QROW + 1].bitcast(f32), 1.0))
            assert link.n == DVE_SETUP
            dve.wait_ge(s["pool_setup"], 2)
            dve.wait_ge(s["wkvbT_psum"], 1)
            for j in range(NI):
                rows = slice(NOPE * j, NOPE * (j + 1))
                last = V.tensor_copy(bd[rows, :, 32 * j:32 * j + R], w1[rows, 0:NI * R].rearrange("p (i l) -> p i l", i=NI))
            last.then_inc(s["bd_ready"], 1)
            V.memset(sq[:], 0.0).then_inc(s["consts_ready"], 1)
            dve.wait_ge(s["act_setup"], 12)
            dve.wait_ge(s["weights_ready"], 1)

            dve.wait_ge(s["x_in"], 32)
            with dve.Fori(0, B) as i:
                link = Chain(dve, s["dve_chain"], DVE_PER, i, DVE_SETUP)
                tile = bass.ds(NT * i, NT)

                def one(t):
                    return bass.ds(NT * i + t, 1)

                def flat(ap):
                    return ap.rearrange("p t c -> p (t c)")

                link(V.tensor_copy(xi[:], x_all[:, tile, :]))
                V.tensor_copy(cx[:], c_all[:, tile, :])
                for t in range(NT):
                    ins = V.bn_stats(st[:, t, :], xi[:, t, :])
                link(ins)
                for t in range(NT):
                    dve.sem_inc(s["dve_passed"], 1)
                    ins = V.bn_aggr(mv[:, t, :], st[:, t, :])
                link(ins)
                link(V.tensor_scalar(vv[:, 0, :], mv[:, :, 1], 1e-5, None, ALU.add))
                link(V.reciprocal(vv[:, 1, :], vv[:, 0, :]))
                link(V.tensor_tensor(vv[:, 1, :], vv[:, 1, :], mv[:, :, 1], ALU.mult))
                V.tensor_scalar(vv[:, 1, :], vv[:, 1, :], 1e-6, None, ALU.add).then_inc(s["var1_ready"], 1)
                dve.wait_ge(s["scale1_ready"], i + 1)
                for t in range(NT):
                    ins = V.tensor_scalar(hx[:, t, :], xi[:, t, :], mv[:, t, 0:1], ss[:, 0, t:t + 1], ALU.subtract, ALU.mult)
                link(ins)
                for t in range(NT):
                    ins = V.scalar_tensor_tensor(out=vx[:, t, :], in0=hx[:, t, :], scalar=ss[:, 1, t:t + 1], in1=normw_b[:], op0=ALU.mult, op1=ALU.mult)
                ins.then_inc(s["front_norm"], 1)
                dve.wait_ge(s["frontT_psum"], i + 1)
                V.tensor_copy(hT[:], w1[:, 0:S]).then_inc(s["frontT_dve"], 1)
                for t in range(NT):
                    dve.wait_ge(s["lx_psum"], NT * i + t + 1)
                    n = P * (t + 1) + S
                    link(V.tensor_reduce(tmp2[:, t:t + 1], [w0, w1][t][:, 0:n], op=ALU.max, axis=AX.X))
                    V.tensor_scalar(nmx[:, t:t + 1], tmp2[:, t:t + 1], -1.0, None, ALU.mult).then_inc(s["nmx_ready"], 1)
                dve.wait_ge(s["pxT_psum"], i + 1)
                V.tensor_copy(pxT[:, 4:7, :], w0[:, 0:3 * P].rearrange("p (k q) -> p k q", k=3)).then_inc(s["pxT_dve"], 1)
                link(V.reciprocal(tmp2[:], rsx[:]))
                dve.wait_ge(s["hx_psum"], i + 1)
                for t in range(NT):
                    ins = V.scalar_tensor_tensor(out=dx[:, t, :], in0=w2[:, P * t:P * (t + 1)], scalar=tmp2[:, t:t + 1], in1=hx[:, t, :], op0=ALU.mult, op1=ALU.subtract)
                link(ins)
                dve.wait_ge(s["thx_ready"], i + 1)
                link(V.scalar_tensor_tensor(out=flat(dx[:]), in0=flat(thx[:]), scalar=1.0, in1=flat(dx[:]), op0=ALU.add, op1=ALU.mult))
                link(V.scalar_tensor_tensor(out=flat(dx[:]), in0=flat(dx[:]), scalar=0.5, in1=flat(hx[:]), op0=ALU.mult, op1=ALU.add))
                link(V.scalar_tensor_tensor(out=flat(xi[:]), in0=flat(dx[:]), scalar=tgx[:, 0:1], in1=flat(xi[:]), op0=ALU.mult, op1=ALU.add))
                for t in range(NT):
                    ins = V.bn_stats(st2[:, t, :], xi[:, t, :])
                link(ins)
                for t in range(NT):
                    dve.sem_inc(s["dve_passed"], 1)
                    ins = V.bn_aggr(mv2[:, t, :], st2[:, t, :])
                link(ins)
                link(V.tensor_scalar(vv2[:, 0, :], mv2[:, :, 1], 1e-5, None, ALU.add))
                link(V.reciprocal(vv2[:, 1, :], vv2[:, 0, :]))
                link(V.tensor_tensor(vv2[:, 1, :], vv2[:, 1, :], mv2[:, :, 1], ALU.mult))
                V.tensor_scalar(vv2[:, 1, :], vv2[:, 1, :], 1e-5, None, ALU.add).then_inc(s["var2_ready"], 1)
                dve.wait_ge(s["scale2_ready"], i + 1)
                for t in range(NT):
                    ins = V.tensor_scalar(h2[:, t, :], xi[:, t, :], mv2[:, t, 0:1], ss2[:, 0, t:t + 1], ALU.subtract, ALU.mult)
                link(ins)
                for t in range(NT):
                    ins = V.tensor_scalar(xn[:, t, :], h2[:, t, :], ss2[:, 1, t:t + 1], None, ALU.mult)
                ins.then_inc(s["xn_ready"], 1)
                dve.wait_ge(s["ckv_psum"], i + 1)
                dve.wait_ge(s["k_lat"], 2 * i + 2)
                kr = w0[:, 0:NT * KD].rearrange("p (t d) -> p t d", t=NT)[:, :, R:KD].rearrange("p t (e d) -> p t e d", e=2)
                V.tensor_tensor(kt1[:], kr, rope_cs[:, :, 0:1, :].to_broadcast([P, NT, 2, HALF]), ALU.mult)
                V.tensor_tensor(kt2[:, :, 0, :], kr[:, :, 1, :], rope_cs[:, :, 1, :], ALU.mult)
                link(V.tensor_tensor(kt2[:, :, 1, :], kr[:, :, 0, :], rope_cs[:, :, 2, :], ALU.mult))
                link(V.tensor_tensor(kf[:, :, R:KD], kt1[:].rearrange("p t e d -> p t (e d)"), kt2[:].rearrange("p t e d -> p t (e d)"), ALU.add))
                V.tensor_copy(ks[:, 0, :, 0:KD], kf[:])
                link(V.tensor_copy(ks[:, 0, :, KD:2 * KD], kf[:]))
                V.tensor_tensor(ks[:, 1, :, 0:KD], kf[:], ks[:, 0, :, 0:KD].bitcast(f32), ALU.subtract)
                V.tensor_tensor(ks[:, 1, :, KD:2 * KD], kf[:], ks[:, 0, :, 0:KD].bitcast(f32), ALU.subtract).then_inc(s["k_split"], 1)
                for t in range(NT):
                    dve.wait_ge(s["q_psum"], NT * i + t + 1)
                    q = w0[:].rearrange("p (h e d) -> p h e d", h=NH, e=2)
                    V.tensor_tensor(q1[:].rearrange("p h e d -> p (h e) d"), q.rearrange("p h e d -> p (h e) d"),
                                    rope_cs[:, t, 0:1, :].to_broadcast([P, 2 * NH, HALF]), ALU.mult)
                    V.tensor_tensor(q2[:, :, 0, :], q[:, :, 1, :], rope_cs[:, t, 1:2, :].to_broadcast([P, NH, HALF]), ALU.mult)
                    V.tensor_tensor(q2[:, :, 1, :], q[:, :, 0, :], rope_cs[:, t, 2:3, :].to_broadcast([P, NH, HALF]), ALU.mult).then_inc(s["q_rope12"], 1)
                n = 0
                for t in range(NT):
                    nk = P * (t + 1)
                    per = 512 // nk
                    for u in range(NH // per):
                        n += 1
                        dve.wait_ge(s["a_psum"], 12 * i + n)
                        V.tensor_reduce(mx[:, t, per * u:per * (u + 1)], pA[n % 2][:].rearrange("p (h k) -> p h k", h=per), op=ALU.max, axis=AX.X).then_inc(s["mx_ready"], 1)
                for t in range(NT):
                    dve.wait_ge(s["pv_psum"], NT * i + t + 1)
                    if t == 1:
                        dve.wait_ge(s["y_psum"], NT * i + 1)
                    link(V.reciprocal(rden[:], pV[:]))
                    dve.sem_inc(s["dve_passed"], 1)
                    link(V.stream_shuffle(den[:], rden[:], [R + k % R for k in range(32)]))
                    V.tensor_tensor(ya[:], pV[:], den[:], ALU.mult).then_inc(s["ya_ready"], 1)
                dve.wait_ge(s["y_psum"], NT * i + NT)
                link(V.tensor_tensor(flat(h2[:]), w1[:, 0:S], flat(h2[:]), ALU.add))
                link(V.tensor_tensor(flat(sq[:]), flat(h2[:]), flat(h2[:]), ALU.mult))
                link(V.tensor_reduce(ms[:], sq[:], op=ALU.add, axis=AX.X))
                V.tensor_scalar(ms[:], ms[:], 1.0 / C, 1e-5, ALU.mult, ALU.add).then_inc(s["var3_ready"], 1)
                dve.wait_ge(s["scale3_ready"], i + 1)
                for t in range(NT):
                    ins = V.tensor_scalar(xn3[:, t, :], h2[:, t, :], r3[:, t:t + 1], None, ALU.mult)
                ins.then_inc(s["xn3_ready"], 1)
                dve.wait_ge(s["lg_psum"], i + 1)
                link(V.tensor_copy(lg[:], w2[:, 0:NT * NE].rearrange("p (t e) -> p t e", t=NT)))
                full = [P, NT, NE]
                rk = rank[:].unsqueeze(1).to_broadcast(full)

                def best(of, m, r1, hot):
                    link(V.tensor_reduce(m[:, :, 0], of[:], op=ALU.max, axis=AX.X))
                    link(V.tensor_tensor(ra[:], of[:], m[:].to_broadcast(full), ALU.is_ge))
                    link(V.tensor_tensor(ra[:], ra[:], rk, ALU.mult))
                    link(V.tensor_reduce(r1[:, :, 0], ra[:], op=ALU.max, axis=AX.X))
                    link(V.tensor_tensor(hot[:], ra[:], r1[:].to_broadcast(full), ALU.is_equal))

                best(lg, m1, ra1, oh1)
                link(V.scalar_tensor_tensor(out=l2[:], in0=oh1[:], scalar=-3.0e38, in1=lg[:], op0=ALU.mult, op1=ALU.add))
                best(l2, m2, rb1, oh2)
                V.tensor_tensor(dm[:], m2[:], m1[:], ALU.subtract).then_inc(s["dm_ready"], 1)
                dve.wait_ge(s["e2_ready"], i + 1)
                link(V.tensor_scalar(p1[:], e2[:], 1.0, 2.0, ALU.add, ALU.mult))
                link(V.reciprocal(p1[:], p1[:]))
                link(V.tensor_tensor(p2[:], p1[:], e2[:], ALU.mult))
                V.tensor_tensor(oh1[:], oh1[:], p1[:].to_broadcast(full), ALU.mult)
                link(V.tensor_tensor(oh2[:], oh2[:], p2[:].to_broadcast(full), ALU.mult))
                V.tensor_tensor(comb[:], oh1[:], oh2[:], ALU.add).then_inc(s["comb_ready"], 1)
                for p in range(NP + 1):
                    rows = P if p < NP else EI
                    w = pA[p % 2]
                    dve.wait_ge(s["th_ready"], (NP + 1) * i + p + 1)
                    link(V.scalar_tensor_tensor(out=s1[0:rows, p, :], in0=th[0:rows, p, :], scalar=1.0, in1=w[0:rows, 0:S], op0=ALU.add, op1=ALU.mult))
                    if p < NP:
                        link(V.tensor_tensor(s1[:, p, :], s1[:, p, :], w[:, S:2 * S], ALU.mult))
                        if p == 0:
                            dve.wait_ge(s["combB_psum"], i + 1)
                        V.tensor_tensor(hid[:, p, :], s1[:, p, :], pB[p // 2][:, S * (p % 2):S * (p % 2 + 1)], ALU.mult).then_inc(s["hid_ready"], 1)
                    else:
                        V.scalar_tensor_tensor(out=hid[0:EI, p, :], in0=s1[0:EI, p, :], scalar=0.5, in1=w[0:EI, S:2 * S], op0=ALU.mult, op1=ALU.mult).then_inc(s["hid_ready"], 1)
                dve.wait_ge(s["moe_psum"], i + 1)
                link(V.tensor_tensor(flat(fin[:]), w0[:, 0:S], flat(h2[:]), ALU.add))
                link(V.scalar_tensor_tensor(out=flat(outt[:]), in0=flat(fin[:]), scalar=tgf[:, 0:1], in1=flat(xi[:]), op0=ALU.mult, op1=ALU.add))
                V.memset(tmp2[:], 0.0).then_inc(s["out_ready"], 1)
                dve.wait_ge(s["out_done"], 16 * (i + 1))
                assert link.n == DVE_PER, link.n


_INS = ["x", "ctx_1024", "g_xattn", "g_ffn"] + ["L0_xattn_" + n for n in ("q_w", "k_w", "norm_w", "gate_w", "gate_b")] + \
    ["L0_ffn_" + n for n in ("w_ln1", "Wq", "Wkva", "Wkvb", "Wo", "w_ln2", "Wgate", "expert_bias", "Wg", "Wu", "Wd", "sWg", "sWu", "sWd")]


def constants():
    freqs = (np.float32(1.0) / np.float32(100000.0) ** (np.arange(0, ROPE, 2, dtype=np.float32) / np.float32(ROPE))).astype(np.float32)
    ang = np.outer(np.arange(S, dtype=np.float32), freqs).astype(np.float32)
    cos, sin = np.cos(ang), np.sin(ang)
    rope = np.stack([cos, -sin, sin], axis=1).reshape(NT, P, 3, HALF).transpose(1, 0, 2, 3)
    k = np.arange(P)
    sel = np.zeros((NE, NP, P), np.float32)
    for e in range(NE):
        sel[e, e // 2, EI * (e % 2):EI * (e % 2 + 1)] = 1.0
    return {
        "c_ident": np.eye(P, dtype=np.float32),
        "c_mask": np.where(k[None, :] > k[:, None], np.float32(NEG), np.float32(0.0)),
        "c_rope": np.ascontiguousarray(rope.astype(np.float32)),
        "c_sel": sel,
        "c_rank": np.tile(np.arange(NE, 0, -1, dtype=np.float32), (P, 1)),
        "c_ones": np.ones((1, P), np.float32),
    }


def kernel(**inputs):
    import concourse.bacc as _bacc
    from concourse.bass_utils import run_bass_kernel_spmd as _run

    nc = _bacc.Bacc("TRN2", target_bir_lowering=False, num_devices=1)
    arrays, aps = {}, {}
    for name, a in [(n, inputs[n]) for n in _INS] + list(constants().items()):
        a = np.ascontiguousarray(a)
        arrays[f"in_{name}"] = a
        aps[name] = nc.dram_tensor(f"in_{name}", a.shape, mybir.dt.from_np(a.dtype), kind="ExternalInput").ap()
    out = nc.dram_tensor("out", (B, S, C), mybir.dt.float32, kind="ExternalOutput").ap()
    build(nc, aps, out)
    r = _run(nc, [arrays], core_ids=[0])
    return r.results[0]["out"]
```

```python
import numpy as np
import concourse.bass as bass
from concourse import mybir
from contextlib import ExitStack

B, S, C = 8, 256, 128
P = 128
NT = S // P
NH, DH, NOPE, ROPE = 16, 64, 32, 32
HALF = ROPE // 2
R = 16
KD = R + ROPE
NI = 4
NE, EI = 8, 64
NP = NE // 2
QROW = 2 * KD
NEG = -1.0e30


def build(nc, t_in, out_d):
    f32, f32r, bf16 = mybir.dt.float32, mybir.dt.float32r, mybir.dt.bfloat16
    ACT, ALU, AX = mybir.ActivationFunctionType, mybir.AluOpType, mybir.AxisListType
    ctx = ExitStack()
    with ctx:
        def sb(name, shape, dt=f32):
            return ctx.enter_context(nc.sbuf_tensor(name, shape, dt))

        def pb(name):
            return ctx.enter_context(nc.psum_tensor(name, [P, 512], f32))

        def sem(name):
            return ctx.enter_context(nc.semaphore(name))

        ident = sb("ident", [P, P])
        mask_f = sb("mask_f", [P, P])
        rope_cs = sb("rope_cs", [P, NT, 3, HALF])
        sel = sb("sel", [NE, NP, P])
        rank = sb("rank", [P, NE])
        ones_row = sb("ones_row", [1, P])
        wq_raw = sb("wq_raw", [P, NH, DH])
        wkva_raw = sb("wkva_raw", [P, KD])
        wkvb_raw = sb("wkvb_raw", [R, NI, NI, NOPE])
        wo_g = sb("wo_g", [P, NI, C])
        xq_w = sb("xq_w", [P, C])
        xk_w = sb("xk_w", [P, C])
        xg_w = sb("xg_w", [P, C])
        gate_b = sb("gate_b", [1, C])
        normw_b = sb("normw_b", [P, C])
        ln1_w = sb("ln1_w", [P, 1])
        ln2_w = sb("ln2_w", [P, 1])
        gx = sb("gx", [P, 1])
        gf = sb("gf", [P, 1])
        ebias = sb("ebias", [1, NE])
        wgate_raw = sb("wgate_raw", [P, NE])
        wg_raw = sb("wg_raw", [P, NE + 1, EI])
        wu_raw = sb("wu_raw", [P, NE + 1, EI])
        wd = sb("wd", [P, NP, C])
        swd = sb("swd", [EI, C])

        identb = sb("identb", [P, P], bf16)
        maskb = sb("maskb", [P, P], bf16)
        ln1_s = sb("ln1_s", [P, 1])
        tgx = sb("tgx", [P, 1])
        tgf = sb("tgf", [P, 1])
        wqn = sb("wqn", [P, NI, NI, NOPE])
        wqnT = sb("wqnT", [P, NI, P])
        bd = sb("bd", [P, NI, NI * R])
        wn = sb("wn", [P, NH, R])
        wr = sb("wr", [P, NH, 2, HALF])
        ka = sb("ka", [P, KD])
        wvo = sb("wvo", [P, 2, C])
        aqk = sb("aqk", [P, C])
        xgT = sb("xgT", [P, C])
        wgate = sb("wgate", [P, NE])
        wg = sb("wg", [P, NE + 1, EI])
        wu = sb("wu", [P, NE + 1, EI])

        x_all = sb("x_all", [P, B * NT, C])
        c_all = sb("c_all", [P, B * NT, C])
        xi = sb("xi", [P, NT, C])
        cx = sb("cx", [P, NT, C])
        h2_all = sb("h2_all", [P, B * NT, C])

        st = sb("st", [P, NT, 6])
        mv = sb("mv", [P, NT, 2])
        nhalf = sb("nhalf", [P, 2, NT])
        vv = sb("vv", [P, 2, NT])
        ss = sb("ss", [P, 2, NT])
        tmp2 = sb("tmp2", [P, NT])
        hx = sb("hx", [P, NT, C])
        vx = sb("vx", [P, NT, C])
        poolT = sb("poolT", [P, 2 * S])
        hqT = sb("hqT", [P, 2, S])
        nmx = sb("nmx", [P, NT])
        rsx = sb("rsx", [P, NT])
        px = sb("px", [P, NT, 2 * S])
        pxT = sb("pxT", [P, 7, P])
        dx = sb("dx", [P, NT, C])
        thx = sb("thx", [P, NT, C])
        st2 = sb("st2", [P, NT, 6])
        mv2 = sb("mv2", [P, NT, 2])
        vv2 = sb("vv2", [P, 2, NT])
        ss2 = sb("ss2", [P, 2, NT])
        xn = sb("xn", [P, NT, C])
        xnT = sb("xnT", [P, S])

        latn = sb("latn", [P, NT, R])
        lat1 = sb("lat1", [P, NT, 2 * R])
        kf = sb("kf", [P, NT, KD])
        kt1 = sb("kt1", [P, NT, 2, HALF])
        kt2 = sb("kt2", [P, NT, 2, HALF])
        ks = sb("ks", [P, 2, NT, P], f32r)
        kTa = sb("kTa", [P, 2, NT, P], f32r)
        kTb = sb("kTb", [P, 2, NT, P], f32r)
        q1 = sb("q1", [P, NH, 2, HALF])
        q2 = sb("q2", [P, NH, 2, HALF])
        qf = sb("qf", [P, NH, KD])
        qs = sb("qs", [P, NH, 2, KD], f32r)
        qT = sb("qT", [P, NT, NH, P], f32r)
        mx = sb("mx", [P, NT, NH])
        mT = sb("mT", [NH, NT, P], f32r)
        pT = sb("pT", [P, 3, NI, 512])
        zs = sb("zs", [P, 512])
        rc = sb("rc", [P, NI, NI, 1])
        yn = sb("yn", [P, NI, NI, R])
        ynT = sb("ynT", [P, 2, P])

        sq = sb("sq", [P, NT, C])
        ms = sb("ms", [P, NT])
        r3 = sb("r3", [P, NT])
        x3 = sb("x3", [P, NT, C])
        xn3 = sb("xn3", [P, NT, C])
        n3T = sb("n3T", [P, S])
        lg = sb("lg", [P, NT, NE])
        m1 = sb("m1", [P, NT, 1])
        m2 = sb("m2", [P, NT, 1])
        ra = sb("ra", [P, NT, NE])
        ra1 = sb("ra1", [P, NT, 1])
        rb1 = sb("rb1", [P, NT, 1])
        oh1 = sb("oh1", [P, NT, NE])
        oh2 = sb("oh2", [P, NT, NE])
        l2 = sb("l2", [P, NT, NE])
        dm = sb("dm", [P, NT, 1])
        e2 = sb("e2", [P, NT, 1])
        p1 = sb("p1", [P, NT, 1])
        p2 = sb("p2", [P, NT, 1])
        comb = sb("comb", [P, NT, NE])
        combT = sb("combT", [NE, S])
        th = sb("th", [P, NP + 1, S])
        s1 = sb("s1", [P, NP + 1, S])
        hid = sb("hid", [P, NP + 1, S])
        fin = sb("fin", [P, NT, C])
        outt = sb("outt", [P, NT, C])

        pA, pB, pV = pb("pA"), pb("pB"), pb("pV")
        wa, wb = pb("wa"), pb("wb")
        wf = pb("wf")
        wm = [pb("wm0"), pb("wm1")]

        names = """consts_in weights_in xw_in x_in consts_ready wqn_ready wqnT_psum wqnT_ready wkvbT_psum
            bd_ready absorb_psum xweights_psum weights_ready act_setup pool_setup
            var1_ready scale1_ready vx_ready poolT_psum poolT_ready hqT_psum hqT_ready lx_psum nmx_ready px_ready
            pxT_psum pxT_ready z_psum thx_ready hx_psum var2_ready scale2_ready xn_ready xnT_psum xnT_ready
            ckv_psum k_lat k_split ksT_psum kTa_ready kTb_ready lat1_ready
            q_psum q_rope q_nope q_full q_high q_low qT_psum qT_ready
            a_psum mx_ready mT_psum mT_ready minus_max_in b_psum exp_ready masked
            pv_psum zs_ready zsT_psum yn_ready ynT_psum ynT_ready y_psum x3_ready var3_ready scale3_ready
            xn3_ready n3T_psum n3T_ready lg_psum dm_ready e2_ready comb_ready combT_psum combT_ready
            combB_psum gu_psum th_ready gu_read hid_ready moe_psum out_ready out_done
            chain_setup chain_front chain_keys chain_attn chain_experts dve_passed pool_passed""".split()
        s = {n: sem(n) for n in names}

        def wait(eng, name, value):
            if not (isinstance(value, int) and value <= 0):
                eng.wait_ge(s[name], value)

        class Chain:

            def __init__(self, eng, name, per, i):
                self.eng, self.name, self.per, self.i, self.n = eng, name, per, i, 0

            def __call__(self, ins):
                self.n += 1
                ins.then_inc(s[self.name], 1)
                self.eng.wait_ge(s[self.name], self.per * self.i + self.n)

        NW, NC_IN, NX = 16 * 20, 16 * 6, 16 * 7
        NU = 12

        def unit(b, t, n):
            return NU * b + NI * t + n + 1

        block = ctx.enter_context(nc.Block())

        def schedule(eng, round_):
            round_(-1)
            round_(0)
            with eng.Fori(1, B - 2) as i:
                round_(i)
            round_(B - 2)
            round_(B - 1)
            round_(B)

        def has(i):
            if not isinstance(i, int):
                return True, True, True, True
            return i + 2 < B, i + 1 < B, 0 <= i < B, i >= 1

        @block.sync
        def _(sp):
            for dst, src in [(ident[:], t_in["c_ident"]), (mask_f[:], t_in["c_mask"]), (rope_cs[:], t_in["c_rope"]),
                             (sel[:], t_in["c_sel"]), (rank[:], t_in["c_rank"]), (ones_row[:], t_in["c_ones"])]:
                sp.dma_start(dst, src).then_inc(s["consts_in"], 16)
            sp.dma_start(x_all[:], t_in["x"].rearrange("b (t p) c -> p (b t) c", p=P)).then_inc(s["x_in"], 16)
            sp.dma_start(c_all[:], t_in["ctx_1024"].rearrange("b (t p) c -> p (b t) c", p=P)).then_inc(s["x_in"], 16)
            sp.dma_start(ln1_w[:], t_in["L0_ffn_w_ln1"].rearrange("(c a) -> c a", a=1)).then_inc(s["weights_in"], 16)
            sp.dma_start(ln2_w[:], t_in["L0_ffn_w_ln2"].rearrange("(c a) -> c a", a=1)).then_inc(s["weights_in"], 16)
            sp.dma_start(wq_raw[:], t_in["L0_ffn_Wq"].rearrange("c (h d) -> c h d", h=NH)).then_inc(s["weights_in"], 16)
            wkvb_v = t_in["L0_ffn_Wkvb"].rearrange("l (j i d) -> i l j d", j=NI, i=NI)
            for m in range(NI):
                sp.dma_start(wkvb_raw[:, m, :, :], wkvb_v[m]).then_inc(s["weights_in"], 16)
            sp.dma_start(wkva_raw[:], t_in["L0_ffn_Wkva"]).then_inc(s["weights_in"], 16)
            wo_v = t_in["L0_ffn_Wo"].rearrange("(j i e d) c -> j e d i c", j=NI, i=NI, e=2)
            for j in range(NI):
                sp.dma_start(wo_g[NOPE * j:NOPE * (j + 1), :, :], wo_v[j, 0]).then_inc(s["weights_in"], 16)
            sp.dma_start(wgate_raw[:], t_in["L0_ffn_Wgate"]).then_inc(s["weights_in"], 16)
            sp.dma_start(ebias[:], t_in["L0_ffn_expert_bias"].rearrange("(a e) -> a e", a=1)).then_inc(s["weights_in"], 16)
            for dst, big, small in [(wg_raw, "L0_ffn_Wg", "L0_ffn_sWg"), (wu_raw, "L0_ffn_Wu", "L0_ffn_sWu")]:
                sp.dma_start(dst[:, 0:NE, :], t_in[big].rearrange("e c i -> c e i")).then_inc(s["weights_in"], 16)
                sp.dma_start(dst[:, NE, :], t_in[small][0]).then_inc(s["weights_in"], 16)
            sp.dma_start(wd[:], t_in["L0_ffn_Wd"].rearrange("(p e) i c -> (e i) p c", e=2)).then_inc(s["weights_in"], 16)
            sp.dma_start(swd[:], t_in["L0_ffn_sWd"][0]).then_inc(s["weights_in"], 16)

            def minus_max(b, t):
                sp.wait_ge(s["mT_ready"], NT * b + t + 1)
                sp.dma_start(qT[QROW:QROW + 1, t, :, :].bitcast(f32), mT[:, t, :].bitcast(f32)).then_inc(s["minus_max_in"], 16)

            def round_(i):
                front, queries, weights, experts = has(i)
                if weights:
                    minus_max(i, 1)
                if queries:
                    minus_max(i + 1, 0)
                if experts:
                    sp.wait_ge(s["out_ready"], i)
                    sp.dma_start(out_d[bass.ds(i - 1, 1), :, :].rearrange("b (t p) c -> p (b t) c", p=P), outt[:]).then_inc(s["out_done"], 16)

            schedule(sp, round_)
            sp.wait_ge(s["out_done"], 16 * B)

        @block.gpsimd
        def _(pool):
            for dst, src in [(xq_w[:], t_in["L0_xattn_q_w"]), (xk_w[:], t_in["L0_xattn_k_w"]), (xg_w[:], t_in["L0_xattn_gate_w"]),
                             (gate_b[:], t_in["L0_xattn_gate_b"].rearrange("(a c) -> a c", a=1)),
                             (normw_b[:], t_in["L0_xattn_norm_w"].partition_broadcast(P)),
                             (gx[:], t_in["g_xattn"].partition_broadcast(P)), (gf[:], t_in["g_ffn"].partition_broadcast(P))]:
                pool.dma_start(dst, src).then_inc(s["xw_in"], 16)
            pool.memset(nhalf[:], -0.5).then_inc(s["pool_setup"], 1)
            pool.memset(bd[:], 0.0).then_inc(s["pool_setup"], 1)
            pool.memset(lat1[:], 1.0).then_inc(s["pool_setup"], 1)
            pool.wait_ge(s["pool_setup"], 3)

            def scale1(b):
                pool.wait_ge(s["var1_ready"], b + 1)
                pool.tensor_tensor(ss[:], vv[:], nhalf[:], ALU.pow).then_inc(s["scale1_ready"], 1)

            def scale2(b):
                pool.wait_ge(s["var2_ready"], b + 1)
                pool.tensor_tensor(ss2[:], vv2[:], nhalf[:], ALU.pow).then_inc(s["scale2_ready"], 1)

            def scale3(b):
                pool.wait_ge(s["var3_ready"], b + 1)
                pool.tensor_tensor(r3[:], ms[:], nhalf[:, 0, :], ALU.pow).then_inc(s["scale3_ready"], 1)

            def rotated(b, t):
                pool.wait_ge(s["q_rope"], NT * b + t + 1)
                pool.tensor_tensor(qf[:, :, R:KD], q1[:].rearrange("p h e d -> p h (e d)"),
                                   q2[:].rearrange("p h e d -> p h (e d)"), ALU.add).then_inc(s["q_full"], 1)

            def low(b, t):
                pool.wait_ge(s["q_high"], NT * b + t + 1)
                pool.tensor_tensor(qs[:, :, 1, :], qf[:], qs[:, :, 0, :].bitcast(f32), ALU.subtract).then_inc(s["q_low"], 1)

            def mask(b, t, g):
                pool.wait_ge(s["exp_ready"], unit(b, t, NI * t + g))
                pool.sem_inc(s["pool_passed"], 1)
                pool.affine_select(out=pT[:, 2 * t, g, :], in_=pT[:, 2 * t, g, :], compare_op=ALU.is_ge, fill=0.0,
                                   base=0, pattern=[[0, NI], [1, P]], channel_multiplier=-1).then_inc(s["masked"], 1)

            def round_(i):
                front, queries, weights, experts = has(i)
                if isinstance(i, int) and i == -1:
                    for b in range(2):
                        scale1(b)
                        scale2(b)
                        if b == 0:
                            for t in range(NT):
                                rotated(0, t)
                                low(0, t)
                    return
                if front:
                    scale1(i + 2)
                if queries:
                    rotated(i + 1, 0)
                    low(i + 1, 0)
                if experts:
                    scale3(i - 1)
                if weights:
                    for g in range(NI):
                        mask(i, 0, g)
                if queries:
                    rotated(i + 1, 1)
                if front:
                    scale2(i + 2)
                if queries:
                    low(i + 1, 1)
                if weights:
                    for g in range(NI):
                        mask(i, 1, g)

            schedule(pool, round_)

        @block.scalar
        def _(act):
            act.wait_ge(s["xw_in"], NX)
            act.activation(tgx[:], gx[:], ACT.Tanh).then_inc(s["act_setup"], 1)
            act.activation(tgf[:], gf[:], ACT.Tanh).then_inc(s["act_setup"], 1)
            act.wait_ge(s["xweights_psum"], 1)
            act.activation(aqk[:], pV[:, 0:C], ACT.Copy, scale=C ** -0.5).then_inc(s["act_setup"], 1)
            act.activation(xgT[:], pV[:, C:2 * C], ACT.Copy).then_inc(s["act_setup"], 1)
            act.wait_ge(s["weights_in"], NW)
            act.activation(ln1_s[:], ln1_w[:], ACT.Copy, scale=DH ** -0.5).then_inc(s["act_setup"], 1)
            act.wait_ge(s["act_setup"], 5)
            act.activation(wqn[:], wq_raw[:, :, 0:NOPE].rearrange("p (j i) d -> p i j d", i=NI), ACT.Copy, scale=ln1_s[:, 0:1]).then_inc(s["wqn_ready"], 1)
            act.activation(wr[:].rearrange("p h e d -> p h d e"), wq_raw[:, :, NOPE:DH].rearrange("p h (d e) -> p h d e", e=2), ACT.Copy, scale=ln1_s[:, 0:1]).then_inc(s["act_setup"], 1)
            act.activation(ka[:, 0:R], wkva_raw[:, 0:R], ACT.Copy, scale=ln1_w[:, 0:1]).then_inc(s["act_setup"], 1)
            act.activation(ka[:, R:KD].rearrange("p (e d) -> p d e", e=2), wkva_raw[:, R:KD].rearrange("p (d e) -> p d e", e=2), ACT.Copy, scale=ln1_w[:, 0:1]).then_inc(s["act_setup"], 1)
            act.activation(wgate[:], wgate_raw[:], ACT.Copy, scale=ln2_w[:, 0:1]).then_inc(s["act_setup"], 1)
            act.activation(wg[:], wg_raw[:], ACT.Copy, scale=ln2_w[:, 0:1]).then_inc(s["act_setup"], 1)
            act.activation(wu[:], wu_raw[:], ACT.Copy, scale=ln2_w[:, 0:1]).then_inc(s["act_setup"], 1)
            act.wait_ge(s["wqnT_psum"], 1)
            act.activation(wqnT[:], wa[:].rearrange("p (i c) -> p i c", i=NI), ACT.Copy).then_inc(s["wqnT_ready"], 1)
            act.wait_ge(s["absorb_psum"], 1)
            act.activation(wn[:].rearrange("p (j i) l -> p i j l", i=NI),
                           wb[:, 0:NH * R].rearrange("p (i j l) -> p i j l", i=NI, j=NI), ACT.Copy).then_inc(s["act_setup"], 1)
            act.activation(wvo[:], wf[:, 0:2 * C].rearrange("p (a c) -> p a c", a=2), ACT.Copy).then_inc(s["weights_ready"], 1)

            def pool_tokens(b):
                act.wait_ge(s["poolT_psum"], b + 1)
                act.activation(poolT[:], wf[:], ACT.Copy).then_inc(s["poolT_ready"], 1)

            def x_queries(b):
                act.wait_ge(s["hqT_psum"], b + 1)
                act.activation(hqT[:], wf[:].rearrange("p (e s) -> p e s", e=2), ACT.Copy).then_inc(s["hqT_ready"], 1)

            def x_weights(b, t):
                act.wait_ge(s["nmx_ready"], NT * b + (1 - t) + 1)
                n = P * (t + 1) + S
                act.activation(px[:, t, 0:n], wf[:, 0:n], ACT.Exp, bias=nmx[:, t:t + 1], accum_out=rsx[:, t:t + 1]).then_inc(s["px_ready"], 1)

            def x_weightsT(b, t):
                act.wait_ge(s["pxT_psum"], NT * b + (1 - t) + 1)
                k0, n = (0, 4) if t == 1 else (4, 3)
                act.activation(pxT[:, k0:k0 + n, :], wf[:, 0:n * P].rearrange("p (k q) -> p k q", k=n), ACT.Copy).then_inc(s["pxT_ready"], 1)

            def x_gate(b):
                act.wait_ge(s["z_psum"], b + 1)
                act.activation(thx[:], wf[:, 0:S].rearrange("p (t c) -> p t c", t=NT), ACT.Tanh, scale=0.5).then_inc(s["thx_ready"], 1)

            def normed(b):
                act.wait_ge(s["xnT_psum"], b + 1)
                act.activation(xnT[:], wf[:, 0:S], ACT.Copy).then_inc(s["xnT_ready"], 1)

            def latent(b):
                act.wait_ge(s["ckv_psum"], b + 1)
                ckv = wm[1][:, 0:NT * KD].rearrange("p (t d) -> p t d", t=NT)
                act.activation(latn[:], ckv[:, :, 0:R], ACT.Copy).then_inc(s["k_lat"], 1)
                act.activation(kf[:, :, 0:R], ckv[:, :, 0:R], ACT.Copy).then_inc(s["k_lat"], 1)

            def keys(b):
                act.wait_ge(s["ksT_psum"], b + 1)
                act.activation(kTa[:], pV[:].rearrange("p (e t q) -> p e t q", e=2, t=NT), ACT.Copy).then_inc(s["kTa_ready"], 1)

            def nope(b, t):
                act.wait_ge(s["q_psum"], NT * b + t + 1)
                act.activation(qf[:, :, 0:R], wb[:, 0:NH * R].rearrange("p (h l) -> p h l", h=NH), ACT.Copy).then_inc(s["q_nope"], 1)

            def high(b, t):
                act.wait_ge(s["q_full"], NT * b + t + 1)
                act.wait_ge(s["q_nope"], NT * b + t + 1)
                act.activation(qs[:, :, 0, :], qf[:], ACT.Copy).then_inc(s["q_high"], 1)

            def queriesT(b, t, g):
                act.wait_ge(s["qT_psum"], NI * (NT * b + t) + g + 1)
                act.activation(qT[0:QROW, t, NI * g:NI * (g + 1), :], [wa, wb][g % 2][0:QROW, :].rearrange("p (h q) -> p h q", h=NI), ACT.Copy).then_inc(s["qT_ready"], 1)

            def minus_max(b, t):
                act.wait_ge(s["mT_psum"], NT * b + t + 1)
                act.activation(mT[:, t, :], [wf, wm[1]][t][0:NH, 0:P], ACT.Copy, scale=-1.0).then_inc(s["mT_ready"], 1)

            def weights_(b, t, kt, g):
                act.wait_ge(s["b_psum"], unit(b, t, NI * kt + g))
                act.activation(pT[:, t + kt, g, :], pB[:], ACT.Exp).then_inc(s["exp_ready"], 1)

            def values(b, t):
                act.wait_ge(s["pv_psum"], NT * b + t + 1)
                act.activation(zs[:], pV[:], ACT.Copy).then_inc(s["zs_ready"], 1)

            def valuesT(b, t):
                act.wait_ge(s["ynT_psum"], NT * b + t + 1)
                act.activation(ynT[:], pV[:, 0:2 * P].rearrange("p (a q) -> p a q", a=2), ACT.Copy).then_inc(s["ynT_ready"], 1)

            def normed3(b):
                act.wait_ge(s["n3T_psum"], b + 1)
                act.activation(n3T[:], wm[0][:, 0:S], ACT.Copy).then_inc(s["n3T_ready"], 1)

            def second_best(b):
                act.wait_ge(s["dm_ready"], b + 1)
                act.activation(e2[:], dm[:], ACT.Exp).then_inc(s["e2_ready"], 1)

            def combT_(b):
                act.wait_ge(s["combT_psum"], b + 1)
                act.activation(combT[:], wm[0][0:NE, 0:S], ACT.Copy).then_inc(s["combT_ready"], 1)

            def gate(b, p):
                rows = P if p < NP else EI
                act.wait_ge(s["gu_psum"], (NP + 1) * b + p + 1)
                act.activation(th[0:rows, p, :], wm[(p + 1) % 2][0:rows, 0:S], ACT.Tanh, scale=0.5).then_inc(s["th_ready"], 1)

            def round_(i):
                front, queries, weights, experts = has(i)
                if isinstance(i, int) and i == -1:
                    for b in range(2):
                        pool_tokens(b)
                        x_queries(b)
                        for t in (1, 0):
                            x_weights(b, t)
                        for t in (1, 0):
                            x_weightsT(b, t)
                        x_gate(b)
                        normed(b)
                        if b == 0:
                            latent(0)
                            nope(0, 0)
                            high(0, 0)
                            keys(0)
                            for g in range(NI):
                                queriesT(0, 0, g)
                            nope(0, 1)
                            high(0, 1)
                            for g in range(NI):
                                queriesT(0, 1, g)
                    minus_max(0, 0)
                    return
                if experts: values(i - 1, 1)
                if queries:
                    nope(i + 1, 0)
                    high(i + 1, 0)
                if front: pool_tokens(i + 2)
                if experts: valuesT(i - 1, 1)
                if front: x_queries(i + 2)
                if queries: latent(i + 1)
                if front: x_weights(i + 2, 1)
                for g in range(NI):
                    if weights: weights_(i, 0, 0, g)
                    if front:
                        if g == 0: x_weights(i + 2, 0)
                        if g == 1: x_weightsT(i + 2, 1)
                        if g == 2: x_weightsT(i + 2, 0)
                        if g == 3: x_gate(i + 2)
                    if weights and g == 0: minus_max(i, 1)
                    if experts:
                        if g == 1: normed3(i - 1)
                        if g == 2: gate(i - 1, 0)
                        if g == 3:
                            second_best(i - 1)
                            gate(i - 1, 1)
                    if queries:
                        if g == 1: keys(i + 1)
                        queriesT(i + 1, 0, g)
                for g in range(NI):
                    if weights: weights_(i, 1, 0, g)
                    if queries:
                        if g == 0: nope(i + 1, 1)
                        if g == 1: high(i + 1, 1)
                    if weights:
                        if g == 1: values(i, 0)
                        if g == 3: valuesT(i, 0)
                    if front and g == 3: normed(i + 2)
                    if experts:
                        if g < 3: gate(i - 1, 2 + g)
                        if g == 3: combT_(i - 1)
                for g in range(NI):
                    if weights: weights_(i, 1, 1, g)
                    if queries:
                        if g == 0: minus_max(i + 1, 0)
                        queriesT(i + 1, 1, g)

            schedule(act, round_)

        @block.tensor
        def _(pe):
            def mm(out, lhsT, rhs, start=True, stop=True):
                return pe.matmul(out, lhsT, rhs, start=start, stop=stop)

            pe.wait_ge(s["consts_in"], NC_IN)
            pe.wait_ge(s["xw_in"], NX)
            mm(pV[:, 0:C], xq_w[:], xk_w[:])
            pe.transpose(pV[:, C:2 * C], xg_w[:], ident[:]).then_inc(s["xweights_psum"], 1)
            pe.wait_ge(s["weights_in"], NW)
            for m in range(NI):
                last = pe.transpose(wb[:, R * m:R * (m + 1)], wkvb_raw[:, m, :, :].rearrange("l j d -> l (j d)"), ident[0:R, 0:R])
            last.then_inc(s["wkvbT_psum"], 1)
            pe.wait_ge(s["wqn_ready"], 1)
            for m in range(NI):
                last = pe.transpose(wa[:, P * m:P * (m + 1)], wqn[:, m, :, :].rearrange("p j d -> p (j d)"), ident[:])
            last.then_inc(s["wqnT_psum"], 1)
            pe.wait_ge(s["bd_ready"], 1)
            pe.wait_ge(s["wqnT_ready"], 1)
            for m in range(NI):
                mm(wb[:, NI * R * m:NI * R * (m + 1)], wqnT[:, m, :], bd[:, m, :])
                half = slice(EI * (m % 2), EI * (m % 2 + 1))
                last = mm(wf[half, C * (m // 2):C * (m // 2 + 1)], bd[:, m, :], wo_g[:, m, :])
            last.then_inc(s["absorb_psum"], 1)
            pe.wait_ge(s["weights_ready"], 1)
            pe.wait_ge(s["consts_ready"], 1)

            def pool_tokens(b):
                pe.wait_ge(s["vx_ready"], b + 1)
                wait(pe, "mT_ready", NT * (b - 2) + 1)
                wait(pe, "xnT_ready", b)
                for t in range(NT):
                    pe.transpose(wf[:, P * t:P * (t + 1)], vx[:, t, :], ident[:])
                    last = pe.transpose(wf[:, S + P * t:S + P * (t + 1)], cx[:, t, :], ident[:])
                last.then_inc(s["poolT_psum"], 1)

            def x_queries(b):
                pe.wait_ge(s["poolT_ready"], b + 1)
                for t in range(NT):
                    pe.transpose(wf[:, P * t:P * (t + 1)], hx[:, t, :], ident[:])
                mm(wf[:, S:2 * S], aqk[:], poolT[:, 0:S]).then_inc(s["hqT_psum"], 1)

            def x_scores(b, t):
                if t == 1:
                    pe.wait_ge(s["hqT_ready"], b + 1)
                    mm(wf[:], hqT[:, 1, P:2 * P], poolT[:], stop=False)
                    mm(wf[:, P:2 * P], identb[:], maskb[:], start=False).then_inc(s["lx_psum"], 1)
                else:
                    pe.wait_ge(s["px_ready"], NT * b + 1)
                    mm(wf[:, 0:P], hqT[:, 1, 0:P], poolT[:, 0:P], stop=False)
                    mm(wf[:, 0:P], identb[:], maskb[:], start=False)
                    mm(wf[:, P:P + S], hqT[:, 1, 0:P], poolT[:, S:2 * S]).then_inc(s["lx_psum"], 1)

            def x_weightsT(b, t):
                pe.wait_ge(s["px_ready"], NT * b + NT)
                if t == 0:
                    pe.wait_ge(s["pxT_ready"], NT * b + 1)
                for k in range(3 + t):
                    last = pe.transpose(wf[:, P * k:P * (k + 1)], px[:, t, P * k:P * (k + 1)], ident[:])
                last.then_inc(s["pxT_psum"], 1)

            def x_gate(b):
                pe.wait_ge(s["pxT_ready"], NT * b + NT)
                for t in range(NT):
                    mm(wf[:, P * t:P * (t + 1)], hqT[:, 0, P * t:P * (t + 1)], xgT[:], stop=False)
                    last = mm(wf[:, P * t:P * (t + 1)], ones_row[:], gate_b[:], start=False)
                last.then_inc(s["z_psum"], 1)

            def x_values(b):
                pe.wait_ge(s["thx_ready"], b + 1)
                vals = [vx[:, 0, :], vx[:, 1, :], cx[:, 0, :], cx[:, 1, :]]
                for k, v in enumerate([vals[0], vals[2], vals[3]]):
                    mm(wf[:, 0:P], pxT[:, 4 + k, :], v, start=k == 0, stop=k == 2)
                for k, v in enumerate(vals):
                    last = mm(wf[:, P:2 * P], pxT[:, k, :], v, start=k == 0, stop=k == 3)
                last.then_inc(s["hx_psum"], 1)

            def normed(b):
                pe.wait_ge(s["xn_ready"], b + 1)
                for t in range(NT):
                    last = pe.transpose(wf[:, P * t:P * (t + 1)], xn[:, t, :], ident[:])
                last.then_inc(s["xnT_psum"], 1)

            def queries_(b, t):
                if t == 0:
                    pe.wait_ge(s["xnT_ready"], b + 1)
                wait(pe, "qT_ready", NI * (NT * b + t))
                q = xnT[:, P * t:P * (t + 1)]
                mm(wa[:], q, wr[:].rearrange("p h e d -> p (h e d)"))
                mm(wb[:, 0:NH * R], q, wn[:].rearrange("p h l -> p (h l)")).then_inc(s["q_psum"], 1)

            def queriesT(b, t, g):
                if g == 0:
                    pe.wait_ge(s["q_low"], NT * b + t + 1)
                if g >= 2:
                    pe.wait_ge(s["qT_ready"], NI * (NT * b + t) + g - 1)
                for h in range(NI):
                    last = pe.transpose([wa, wb][g % 2][0:QROW, P * h:P * (h + 1)], qs[:, NI * g + h, :, :].bitcast(f32).rearrange("p e d -> p (e d)"), ident[:])
                last.then_inc(s["qT_psum"], 1)

            def latent(b):
                pe.wait_ge(s["xnT_ready"], b + 1)
                wait(pe, "hid_ready", 2 * (b - 2))
                for t in range(NT):
                    last = mm(wm[1][:, KD * t:KD * (t + 1)], xnT[:, P * t:P * (t + 1)], ka[:])
                last.then_inc(s["ckv_psum"], 1)

            def keys(b):
                pe.wait_ge(s["k_split"], b + 1)
                wait(pe, "x3_ready", NT * (b - 1))
                for e in range(2):
                    for t in range(NT):
                        last = pe.transpose(pV[:, (NT * e + t) * P:(NT * e + t + 1) * P], ks[:, e, t, :].bitcast(f32), ident[:])
                last.then_inc(s["ksT_psum"], 1)

            def maxima(b, t, u):
                nk = P * (t + 1)
                per = 512 // nk
                if t == 0:
                    pe.wait_ge(s["kTa_ready"], b + 1)
                pe.wait_ge(s["qT_ready"], NI * (NT * b + t) + (per * u) // NI + 1)
                wait(pe, "mx_ready", unit(b, t, u) - 1)
                for h in range(per):
                    mm(pA[:, nk * h:nk * (h + 1)], qT[0:QROW, t, per * u + h, :],
                       kTa[0:QROW, 0, 0:t + 1, :].rearrange("p t q -> p (t q)"), start=h == 0, stop=False)
                mm(pA[:].rearrange("p (h k) -> p h k", h=per)[:, :, P * t:P * (t + 1)], identb[:],
                   maskb[:].unsqueeze(1).to_broadcast([P, per, P]), start=False).then_inc(s["a_psum"], 1)

            def minus_max(b, t):
                pe.wait_ge(s["mx_ready"], unit(b, t, NI * (t + 1) - 1))
                if t == 0:
                    pe.wait_ge(s["xnT_ready"], min(b + 2, B) if isinstance(b, int) else b + 2)
                else:
                    wait(pe, "k_split", min(b + 2, B) if isinstance(b, int) else b + 2)
                pe.transpose([wf, wm[1]][t][0:NH, 0:P], mx[:, t, :], ident[:]).then_inc(s["mT_psum"], 1)

            def weights_(b, t, kt, g):
                if kt == 0 and g == 0:
                    pe.wait_ge(s["minus_max_in"], 16 * (NT * b + t + 1))
                    if t == 0:
                        pe.wait_ge(s["kTb_ready"], b + 1)
                wait(pe, "exp_ready", unit(b, t, NI * kt + g) - 1)
                q = qT[0:QROW + 1, t, NI * g:NI * (g + 1), :].rearrange("p h q -> p (h q)")
                mm(pB[:], kTb[0:QROW + 1, 0, kt, :], q, stop=False)
                mm(pB[:], kTb[0:QROW + 1, 1, kt, :], q, start=False).then_inc(s["b_psum"], 1)

            def values(b, t):
                if t == 0:
                    pe.wait_ge(s["lat1_ready"], b + 1)
                    pe.wait_ge(s["kTa_ready"], min(b + 2, B) if isinstance(b, int) else b + 2)
                wait(pe, "x3_ready", NT * b + t)
                pe.wait_ge(s["masked"], NI * (NT * b + t + 1))
                for kt in range(t + 1):
                    for g in range(NI):
                        last = mm(pV[32 * g:32 * (g + 1), :], lat1[:, kt, :], pT[:, t + kt, g, :], start=kt == 0, stop=kt == t)
                last.then_inc(s["pv_psum"], 1)

            def values_by_query(b, t):
                pe.wait_ge(s["zs_ready"], NT * b + t + 1)
                for m in range(NI):
                    last = pe.transpose(pV[:, P * m:P * (m + 1)], zs[:, P * m:P * (m + 1)], ident[:])
                last.then_inc(s["zsT_psum"], 1)

            def valuesT(b, t):
                pe.wait_ge(s["yn_ready"], NT * b + t + 1)
                y = yn[:].rearrange("p m j l -> p (m j l)")
                for a in range(2):
                    last = pe.transpose(pV[:, P * a:P * (a + 1)], y[:, P * a:P * (a + 1)], ident[:])
                last.then_inc(s["ynT_psum"], 1)

            def project(b, t):
                pe.wait_ge(s["ynT_ready"], NT * b + t + 1)
                for a in range(2):
                    last = mm(pV[:, 0:C], ynT[:, a, :], wvo[:, a, :], start=a == 0, stop=a == 1)
                last.then_inc(s["y_psum"], 1)

            def normed3(b):
                pe.wait_ge(s["xn3_ready"], b + 1)
                for t in range(NT):
                    last = pe.transpose(wm[0][:, P * t:P * (t + 1)], xn3[:, t, :], ident[:])
                last.then_inc(s["n3T_psum"], 1)

            def router(b):
                pe.wait_ge(s["n3T_ready"], b + 1)
                for t in range(NT):
                    mm(wm[0][:, NE * t:NE * (t + 1)], n3T[:, P * t:P * (t + 1)], wgate[:], stop=False)
                    last = mm(wm[0][:, NE * t:NE * (t + 1)], ones_row[:], ebias[:], start=False)
                last.then_inc(s["lg_psum"], 1)

            def gate_up(b, p):
                rows = P if p < NP else EI
                w = wm[(p + 1) % 2]
                if p == 0:
                    wait(pe, "mT_ready", NT * (b + 1) + 2 if not isinstance(b, int) else min(NT * (b + 1) + 2, NT * B))
                if p == 1:
                    pe.wait_ge(s["dm_ready"], b + 1)
                if p >= 2:
                    pe.wait_ge(s["gu_read"], (NP + 1) * b + p - 1)
                last_e = min(2 * p + 2, NE + 1)
                mm(w[0:rows, 0:S], wg[:, 2 * p:last_e, :].rearrange("p e i -> p (e i)"), n3T[:])
                mm(w[0:rows, S:2 * S], wu[:, 2 * p:last_e, :].rearrange("p e i -> p (e i)"), n3T[:]).then_inc(s["gu_psum"], 1)

            def combT_(b):
                pe.wait_ge(s["comb_ready"], b + 1)
                pe.wait_ge(s["gu_read"], (NP + 1) * b + NP)
                for t in range(NT):
                    last = pe.transpose(wm[0][0:NE, P * t:P * (t + 1)], comb[:, t, :], ident[:])
                last.then_inc(s["combT_psum"], 1)

            def spread(b):
                pe.wait_ge(s["combT_ready"], b + 1)
                pe.wait_ge(s["gu_read"], (NP + 1) * (b + 1))
                for q in range(NP):
                    last = mm(wm[q // 2][:, S * (q % 2):S * (q % 2 + 1)], sel[:, q, :], combT[:])
                    if q % 2:
                        last.then_inc(s["combB_psum"], 1)

            def down(b):
                pe.wait_ge(s["hid_ready"], 2 * (b + 1))
                w = wm[0]
                for t in range(NT):
                    for p in range(NP):
                        mm(w[:, P * t:P * (t + 1)], hid[:, p, P * t:P * (t + 1)], wd[:, p, :], start=p == 0, stop=False)
                    last = mm(w[:, P * t:P * (t + 1)], hid[0:EI, NP, P * t:P * (t + 1)], swd[:], start=False)
                last.then_inc(s["moe_psum"], 1)

            def round_(i):
                front, queries, weights, experts = has(i)
                if isinstance(i, int) and i == -1:
                    for b in range(2):
                        pool_tokens(b)
                        x_queries(b)
                        for t in (1, 0):
                            x_scores(b, t)
                        for t in (1, 0):
                            x_weightsT(b, t)
                        x_gate(b)
                        x_values(b)
                        normed(b)
                        if b == 0:
                            latent(0)
                            queries_(0, 0)
                            keys(0)
                            for g in range(NI):
                                queriesT(0, 0, g)
                            queries_(0, 1)
                            for g in range(NI):
                                queriesT(0, 1, g)
                            for g in range(NI):
                                maxima(0, 0, g)
                    minus_max(0, 0)
                    return
                if weights: maxima(i, 1, 0)
                if experts: values(i - 1, 1)
                if queries: queries_(i + 1, 0)
                if weights: maxima(i, 1, 1)
                if weights: maxima(i, 1, 2)
                if experts: values_by_query(i - 1, 1)
                if front: pool_tokens(i + 2)
                if weights: maxima(i, 1, 3)
                if weights: maxima(i, 1, 4)
                if experts: valuesT(i - 1, 1)
                if front: x_queries(i + 2)
                if queries: latent(i + 1)
                if weights: maxima(i, 1, 5)
                if weights: maxima(i, 1, 6)
                if experts: project(i - 1, 1)
                if front: x_scores(i + 2, 1)
                if weights: maxima(i, 1, 7)
                for g in range(NI):
                    if weights: weights_(i, 0, 0, g)
                    if front:
                        if g == 0: x_scores(i + 2, 0)
                        if g == 1: x_weightsT(i + 2, 1)
                        if g == 2: x_weightsT(i + 2, 0)
                        if g == 3: x_gate(i + 2)
                    if weights and g == 0: minus_max(i, 1)
                    if experts:
                        if g == 1: normed3(i - 1)
                        if g == 2:
                            router(i - 1)
                            gate_up(i - 1, 0)
                        if g == 3: gate_up(i - 1, 1)
                    if queries:
                        if g == 1: keys(i + 1)
                        queriesT(i + 1, 0, g)
                for g in range(NI):
                    if weights: weights_(i, 1, 0, g)
                    if queries and g == 0: queries_(i + 1, 1)
                    if front and g == 0: x_values(i + 2)
                    if weights:
                        if g == 1: values(i, 0)
                        if g == 2: values_by_query(i, 0)
                        if g == 3: valuesT(i, 0)
                    if front and g == 3: normed(i + 2)
                    if experts:
                        if g < 3: gate_up(i - 1, 2 + g)
                        if g == 3: combT_(i - 1)
                    if queries: maxima(i + 1, 0, g)
                for g in range(NI):
                    if weights: weights_(i, 1, 1, g)
                    if weights and g == 0: project(i, 0)
                    if experts:
                        if g == 0: spread(i - 1)
                        if g == 2: down(i - 1)
                    if queries:
                        if g == 0: minus_max(i + 1, 0)
                        queriesT(i + 1, 1, g)

            schedule(pe, round_)

        @block.vector
        def _(dve):
            V = nc.vector
            dve.wait_ge(s["consts_in"], NC_IN)
            V.tensor_copy(identb[:], ident[:])
            V.tensor_copy(maskb[:], mask_f[:])
            V.memset(ks[:].bitcast(f32), 0.0)
            link = Chain(dve, "chain_setup", 2, 0)
            link(V.memset(sq[:], 0.0))
            link(V.memset(ks[:, 0, :, QROW:QROW + 1].bitcast(f32), 1.0))
            dve.wait_ge(s["pool_setup"], 3)
            dve.wait_ge(s["wkvbT_psum"], 1)
            for j in range(NI):
                rows = slice(NOPE * j, NOPE * (j + 1))
                last = V.tensor_copy(bd[rows, :, R * j:R * (j + 1)], wb[rows, 0:NI * R].rearrange("p (i l) -> p i l", i=NI))
            last.then_inc(s["bd_ready"], 1)
            V.memset(sq[:], 0.0).then_inc(s["consts_ready"], 1)
            dve.wait_ge(s["act_setup"], 12)
            dve.wait_ge(s["weights_ready"], 1)
            dve.wait_ge(s["x_in"], 32)

            def flat(ap):
                return ap.rearrange("p t c -> p (t c)")

            def tiles(b):
                return bass.ds(NT * b, NT)

            def one(b, t):
                return bass.ds(NT * b + t, 1)

            front_chain, PER_FRONT = {}, 21
            expert_chain, PER_EXPERTS = {}, 26

            def norms(b):
                link = front_chain[0] = Chain(dve, "chain_front", PER_FRONT, b)
                V.tensor_copy(cx[:], c_all[:, tiles(b), :])
                link(V.tensor_copy(xi[:], x_all[:, tiles(b), :]))
                for t in range(NT):
                    ins = V.bn_stats(st[:, t, :], xi[:, t, :])
                link(ins)
                for t in range(NT):
                    dve.sem_inc(s["dve_passed"], 1)
                    ins = V.bn_aggr(mv[:, t, :], st[:, t, :])
                link(ins)
                link(V.tensor_scalar(vv[:, 0, :], mv[:, :, 1], 1e-5, None, ALU.add))
                link(V.reciprocal(vv[:, 1, :], vv[:, 0, :]))
                link(V.tensor_tensor(vv[:, 1, :], vv[:, 1, :], mv[:, :, 1], ALU.mult))
                V.tensor_scalar(vv[:, 1, :], vv[:, 1, :], 1e-6, None, ALU.add).then_inc(s["var1_ready"], 1)

            def scaled(b):
                link = front_chain[0]
                dve.wait_ge(s["scale1_ready"], b + 1)
                for t in range(NT):
                    ins = V.tensor_scalar(hx[:, t, :], xi[:, t, :], mv[:, t, 0:1], ss[:, 0, t:t + 1], ALU.subtract, ALU.mult)
                link(ins)
                for t in range(NT):
                    ins = V.scalar_tensor_tensor(out=vx[:, t, :], in0=hx[:, t, :], scalar=ss[:, 1, t:t + 1], in1=normw_b[:], op0=ALU.mult, op1=ALU.mult)
                ins.then_inc(s["vx_ready"], 1)

            def x_max(b, t):
                link = front_chain[0]
                dve.wait_ge(s["lx_psum"], NT * b + (1 - t) + 1)
                n = P * (t + 1) + S
                link(V.tensor_reduce(tmp2[:, t:t + 1], wf[:, 0:n], op=ALU.max, axis=AX.X))
                V.tensor_scalar(nmx[:, t:t + 1], tmp2[:, t:t + 1], -1.0, None, ALU.mult).then_inc(s["nmx_ready"], 1)

            def mix(b):
                link = front_chain[0]
                dve.wait_ge(s["px_ready"], NT * (b + 1))
                link(V.reciprocal(tmp2[:], rsx[:]))
                dve.wait_ge(s["hx_psum"], b + 1)
                for t in range(NT):
                    ins = V.scalar_tensor_tensor(out=dx[:, t, :], in0=wf[:, P * t:P * (t + 1)], scalar=tmp2[:, t:t + 1], in1=hx[:, t, :], op0=ALU.mult, op1=ALU.subtract)
                link(ins)
                link(V.scalar_tensor_tensor(out=flat(dx[:]), in0=flat(thx[:]), scalar=1.0, in1=flat(dx[:]), op0=ALU.add, op1=ALU.mult))
                link(V.scalar_tensor_tensor(out=flat(dx[:]), in0=flat(dx[:]), scalar=0.5, in1=flat(hx[:]), op0=ALU.mult, op1=ALU.add))
                link(V.scalar_tensor_tensor(out=flat(xi[:]), in0=flat(dx[:]), scalar=tgx[:, 0:1], in1=flat(xi[:]), op0=ALU.mult, op1=ALU.add))
                for t in range(NT):
                    ins = V.bn_stats(st2[:, t, :], xi[:, t, :])
                link(ins)
                for t in range(NT):
                    dve.sem_inc(s["dve_passed"], 1)
                    ins = V.bn_aggr(mv2[:, t, :], st2[:, t, :])
                link(ins)
                link(V.tensor_scalar(vv2[:, 0, :], mv2[:, :, 1], 1e-5, None, ALU.add))
                link(V.reciprocal(vv2[:, 1, :], vv2[:, 0, :]))
                link(V.tensor_tensor(vv2[:, 1, :], vv2[:, 1, :], mv2[:, :, 1], ALU.mult))
                V.tensor_scalar(vv2[:, 1, :], vv2[:, 1, :], 1e-5, None, ALU.add).then_inc(s["var2_ready"], 1)
                V.tensor_copy(x_all[:, tiles(b), :], xi[:])

            def normed(b):
                link = front_chain[0]
                dve.wait_ge(s["scale2_ready"], b + 1)
                for t in range(NT):
                    ins = V.tensor_scalar(dx[:, t, :], xi[:, t, :], mv2[:, t, 0:1], ss2[:, 0, t:t + 1], ALU.subtract, ALU.mult)
                link(ins)
                for t in range(NT):
                    ins = V.tensor_scalar(xn[:, t, :], dx[:, t, :], ss2[:, 1, t:t + 1], None, ALU.mult)
                ins.then_inc(s["xn_ready"], 1)
                link(V.tensor_copy(h2_all[:, tiles(b), :], dx[:]))
                assert link.n == PER_FRONT, link.n

            def rotate_keys(b):
                link = Chain(dve, "chain_keys", 3, b)
                dve.wait_ge(s["k_lat"], 2 * b + 2)
                kr = wm[1][:, 0:NT * KD].rearrange("p (t d) -> p t d", t=NT)[:, :, R:KD].rearrange("p t (e d) -> p t e d", e=2)
                V.tensor_tensor(kt1[:], kr, rope_cs[:, :, 0:1, :].to_broadcast([P, NT, 2, HALF]), ALU.mult)
                V.tensor_tensor(kt2[:, :, 0, :], kr[:, :, 1, :], rope_cs[:, :, 1, :], ALU.mult)
                link(V.tensor_tensor(kt2[:, :, 1, :], kr[:, :, 0, :], rope_cs[:, :, 2, :], ALU.mult))
                link(V.tensor_tensor(kf[:, :, R:KD], kt1[:].rearrange("p t e d -> p t (e d)"), kt2[:].rearrange("p t e d -> p t (e d)"), ALU.add))
                V.tensor_copy(ks[:, 0, :, 0:KD], kf[:])
                link(V.tensor_copy(ks[:, 0, :, KD:2 * KD], kf[:]))
                V.tensor_tensor(ks[:, 1, :, 0:KD], kf[:], ks[:, 0, :, 0:KD].bitcast(f32), ALU.subtract)
                V.tensor_tensor(ks[:, 1, :, KD:2 * KD], kf[:], ks[:, 0, :, 0:KD].bitcast(f32), ALU.subtract).then_inc(s["k_split"], 1)

            def keys_turn(b):
                wait(dve, "b_psum", NU * b)
                dve.wait_ge(s["kTa_ready"], b + 1)
                V.tensor_copy(kTb[:], kTa[:].bitcast(f32)).then_inc(s["kTb_ready"], 1)

            def latent_turn(b):
                wait(dve, "pv_psum", NT * b)
                dve.wait_ge(s["k_lat"], 2 * b + 2)
                V.tensor_copy(lat1[:, :, 0:R], latn[:]).then_inc(s["lat1_ready"], 1)

            def rotate(b, t):
                dve.wait_ge(s["q_psum"], NT * b + t + 1)
                q = wa[:].rearrange("p (h e d) -> p h e d", h=NH, e=2)
                V.tensor_tensor(q1[:].rearrange("p h e d -> p (h e) d"), q.rearrange("p h e d -> p (h e) d"),
                                rope_cs[:, t, 0:1, :].to_broadcast([P, 2 * NH, HALF]), ALU.mult)
                V.tensor_tensor(q2[:, :, 0, :], q[:, :, 1, :], rope_cs[:, t, 1:2, :].to_broadcast([P, NH, HALF]), ALU.mult)
                V.tensor_tensor(q2[:, :, 1, :], q[:, :, 0, :], rope_cs[:, t, 2:3, :].to_broadcast([P, NH, HALF]), ALU.mult).then_inc(s["q_rope"], 1)

            def maxima(b, t, u):
                per = NI // (t + 1)
                dve.wait_ge(s["a_psum"], unit(b, t, u))
                V.tensor_reduce(mx[:, t, per * u:per * (u + 1)], pA[:].rearrange("p (h k) -> p h k", h=per), op=ALU.max, axis=AX.X).then_inc(s["mx_ready"], 1)

            def normalise(b, t):
                link = Chain(dve, "chain_attn", NT, b)
                link.n = t
                dve.wait_ge(s["zsT_psum"], NT * b + t + 1)
                z = pV[:].rearrange("p (m j l) -> p m j l", m=NI, j=NI)
                link(V.reciprocal(rc[:], z[:, :, :, R:R + 1]))
                V.tensor_tensor(yn[:], z[:, :, :, 0:R], rc[:].to_broadcast([P, NI, NI, R]), ALU.mult).then_inc(s["yn_ready"], 1)

            def add_attention(b, t):
                dve.wait_ge(s["y_psum"], NT * b + t + 1)
                V.tensor_tensor(h2_all[:, one(b, t), :], pV[:, 0:C].unsqueeze(1), h2_all[:, one(b, t), :], ALU.add).then_inc(s["x3_ready"], 1)

            def variance3(b):
                link = expert_chain[0] = Chain(dve, "chain_experts", PER_EXPERTS, b)
                dve.wait_ge(s["x3_ready"], NT * (b + 1))
                link(V.tensor_copy(x3[:], h2_all[:, tiles(b), :]))
                link(V.tensor_tensor(flat(sq[:]), flat(x3[:]), flat(x3[:]), ALU.mult))
                link(V.tensor_reduce(ms[:], sq[:], op=ALU.add, axis=AX.X))
                V.tensor_scalar(ms[:], ms[:], 1.0 / C, 1e-5, ALU.mult, ALU.add).then_inc(s["var3_ready"], 1)

            def normed3(b):
                dve.wait_ge(s["scale3_ready"], b + 1)
                for t in range(NT):
                    ins = V.tensor_scalar(xn3[:, t, :], x3[:, t, :], r3[:, t:t + 1], None, ALU.mult)
                ins.then_inc(s["xn3_ready"], 1)

            full = [P, NT, NE]

            def two_best(b):
                link = expert_chain[0]
                dve.wait_ge(s["lg_psum"], b + 1)
                link(V.tensor_copy(lg[:], wm[0][:, 0:NT * NE].rearrange("p (t e) -> p t e", t=NT)))

                def best(of, m, r1, hot):
                    link(V.tensor_reduce(m[:, :, 0], of[:], op=ALU.max, axis=AX.X))
                    link(V.tensor_tensor(ra[:], of[:], m[:].to_broadcast(full), ALU.is_ge))
                    link(V.tensor_tensor(ra[:], ra[:], rank[:].unsqueeze(1).to_broadcast(full), ALU.mult))
                    link(V.tensor_reduce(r1[:, :, 0], ra[:], op=ALU.max, axis=AX.X))
                    link(V.tensor_tensor(hot[:], ra[:], r1[:].to_broadcast(full), ALU.is_equal))

                best(lg, m1, ra1, oh1)
                link(V.scalar_tensor_tensor(out=l2[:], in0=oh1[:], scalar=-3.0e38, in1=lg[:], op0=ALU.mult, op1=ALU.add))
                best(l2, m2, rb1, oh2)
                V.tensor_tensor(dm[:], m2[:], m1[:], ALU.subtract).then_inc(s["dm_ready"], 1)

            def combine_weights(b):
                link = expert_chain[0]
                dve.wait_ge(s["e2_ready"], b + 1)
                link(V.tensor_scalar(p1[:], e2[:], 1.0, 2.0, ALU.add, ALU.mult))
                link(V.reciprocal(p1[:], p1[:]))
                link(V.tensor_tensor(p2[:], p1[:], e2[:], ALU.mult))
                V.tensor_tensor(oh1[:], oh1[:], p1[:].to_broadcast(full), ALU.mult)
                link(V.tensor_tensor(oh2[:], oh2[:], p2[:].to_broadcast(full), ALU.mult))
                V.tensor_tensor(comb[:], oh1[:], oh2[:], ALU.add).then_inc(s["comb_ready"], 1)

            def inner(b, p):
                link = expert_chain[0]
                rows = P if p < NP else EI
                w = wm[(p + 1) % 2]
                dve.wait_ge(s["th_ready"], (NP + 1) * b + p + 1)
                link(V.scalar_tensor_tensor(out=s1[0:rows, p, :], in0=th[0:rows, p, :], scalar=1.0, in1=w[0:rows, 0:S], op0=ALU.add, op1=ALU.mult))
                if p < NP:
                    V.tensor_tensor(s1[:, p, :], s1[:, p, :], w[:, S:2 * S], ALU.mult).then_inc(s["gu_read"], 1)
                else:
                    V.scalar_tensor_tensor(out=hid[0:EI, p, :], in0=s1[0:EI, p, :], scalar=0.5, in1=w[0:EI, S:2 * S], op0=ALU.mult, op1=ALU.mult).then_inc(s["gu_read"], 1)

            def weigh(b):
                dve.wait_ge(s["gu_read"], (NP + 1) * (b + 1))
                for a in range(2):
                    dve.wait_ge(s["combB_psum"], 2 * b + a + 1)
                    V.tensor_tensor(hid[:, 2 * a:2 * a + 2, :], s1[:, 2 * a:2 * a + 2, :], wm[a][:].rearrange("p (e s) -> p e s", e=2), ALU.mult).then_inc(s["hid_ready"], 1)

            def finish(b):
                link = expert_chain[0]
                dve.wait_ge(s["moe_psum"], b + 1)
                link(V.tensor_tensor(flat(fin[:]), wm[0][:, 0:S], flat(x3[:]), ALU.add))
                wait(dve, "out_done", 16 * b)
                link(V.scalar_tensor_tensor(out=outt[:], in0=fin[:], scalar=tgf[:, 0:1], in1=x_all[:, tiles(b), :], op0=ALU.mult, op1=ALU.add))
                dve.sem_inc(s["out_ready"], 1)
                assert link.n == PER_EXPERTS, link.n

            def round_(i):
                front, queries, weights, experts = has(i)
                if isinstance(i, int) and i == -1:
                    for b in range(2):
                        norms(b)
                        scaled(b)
                        for t in (1, 0):
                            x_max(b, t)
                        mix(b)
                        normed(b)
                        if b == 0:
                            rotate_keys(0)
                            rotate(0, 0)
                            rotate(0, 1)
                            for g in range(NI):
                                maxima(0, 0, g)
                    return
                if weights:
                    keys_turn(i)
                    maxima(i, 1, 0)
                if front: norms(i + 2)
                if queries: rotate(i + 1, 0)
                if front: scaled(i + 2)
                if weights: maxima(i, 1, 1)
                if weights:
                    maxima(i, 1, 2)
                    latent_turn(i)
                if experts: normalise(i - 1, 1)
                if weights: maxima(i, 1, 3)
                if weights: maxima(i, 1, 4)
                if queries: rotate_keys(i + 1)
                if weights: maxima(i, 1, 5)
                if weights: maxima(i, 1, 6)
                if experts:
                    add_attention(i - 1, 1)
                    variance3(i - 1)
                if front: x_max(i + 2, 1)
                if weights: maxima(i, 1, 7)
                if experts: normed3(i - 1)
                if front: x_max(i + 2, 0)
                if experts:
                    two_best(i - 1)
                    inner(i - 1, 0)
                    inner(i - 1, 1)
                if queries: rotate(i + 1, 1)
                if front: mix(i + 2)
                if experts: inner(i - 1, 2)
                if queries: maxima(i + 1, 0, 0)
                if front: normed(i + 2)
                if experts:
                    combine_weights(i - 1)
                    inner(i - 1, 3)
                if queries: maxima(i + 1, 0, 1)
                if weights: normalise(i, 0)
                if experts: inner(i - 1, 4)
                if queries:
                    maxima(i + 1, 0, 2)
                    maxima(i + 1, 0, 3)
                if weights: add_attention(i, 0)
                if experts:
                    weigh(i - 1)
                    finish(i - 1)

            schedule(dve, round_)


_INS = ["x", "ctx_1024", "g_xattn", "g_ffn"] + ["L0_xattn_" + n for n in ("q_w", "k_w", "norm_w", "gate_w", "gate_b")] + \
    ["L0_ffn_" + n for n in ("w_ln1", "Wq", "Wkva", "Wkvb", "Wo", "w_ln2", "Wgate", "expert_bias", "Wg", "Wu", "Wd", "sWg", "sWu", "sWd")]


def constants():
    freqs = (np.float32(1.0) / np.float32(100000.0) ** (np.arange(0, ROPE, 2, dtype=np.float32) / np.float32(ROPE))).astype(np.float32)
    ang = np.outer(np.arange(S, dtype=np.float32), freqs).astype(np.float32)
    cos, sin = np.cos(ang), np.sin(ang)
    rope = np.stack([cos, -sin, sin], axis=1).reshape(NT, P, 3, HALF).transpose(1, 0, 2, 3)
    k = np.arange(P)
    sel = np.zeros((NE, NP, P), np.float32)
    for e in range(NE):
        sel[e, e // 2, EI * (e % 2):EI * (e % 2 + 1)] = 1.0
    return {
        "c_ident": np.eye(P, dtype=np.float32),
        "c_mask": np.where(k[None, :] > k[:, None], np.float32(NEG), np.float32(0.0)),
        "c_rope": np.ascontiguousarray(rope.astype(np.float32)),
        "c_sel": sel,
        "c_rank": np.tile(np.arange(NE, 0, -1, dtype=np.float32), (P, 1)),
        "c_ones": np.ones((1, P), np.float32),
    }


def kernel(**inputs):
    import concourse.bacc as _bacc
    from concourse.bass_utils import run_bass_kernel_spmd as _run

    nc = _bacc.Bacc("TRN2", target_bir_lowering=False, num_devices=1)
    arrays, aps = {}, {}
    for name, a in [(n, inputs[n]) for n in _INS] + list(constants().items()):
        a = np.ascontiguousarray(a)
        arrays[f"in_{name}"] = a
        aps[name] = nc.dram_tensor(f"in_{name}", a.shape, mybir.dt.from_np(a.dtype), kind="ExternalInput").ap()
    out = nc.dram_tensor("out", (B, S, C), mybir.dt.float32, kind="ExternalOutput").ap()
    build(nc, aps, out)
    r = _run(nc, [arrays], core_ids=[0])
    return r.results[0]["out"]
```

```python
import numpy as np
import concourse.bass as bass
from concourse import mybir
from contextlib import ExitStack

B, S, C = 8, 256, 128
P = 128
NT = S // P
NH, DH, NOPE, ROPE = 16, 64, 32, 32
HALF = ROPE // 2
R = 16
KD = R + ROPE
NI = 4
NE, EI = 8, 64
NP = NE // 2
QROW = 2 * KD
NCONST = 2 * P + NT * 3 * HALF + NE
NEG = -1.0e30


def build(nc, t_in, out_d):
    f32, f32r, bf16 = mybir.dt.float32, mybir.dt.float32r, mybir.dt.bfloat16
    ACT, ALU, AX = mybir.ActivationFunctionType, mybir.AluOpType, mybir.AxisListType
    ctx = ExitStack()
    with ctx:
        def sb(name, shape, dt=f32):
            return ctx.enter_context(nc.sbuf_tensor(name, shape, dt))

        def pb(name):
            return ctx.enter_context(nc.psum_tensor(name, [P, 512], f32))

        def sem(name):
            return ctx.enter_context(nc.semaphore(name))

        consts = sb("consts", [P, NCONST])
        ident, mask_f = consts[:, 0:P], consts[:, P:2 * P]
        rope_cs = consts[:, 2 * P:2 * P + NT * 3 * HALF].rearrange("p (t e d) -> p t e d", t=NT, e=3)
        number = consts[:, NCONST - NE:NCONST]
        sel_f = sb("sel_f", [2 * NE, NP, P])
        wq_raw = sb("wq_raw", [P, NH, DH])
        wkva_raw = sb("wkva_raw", [P, KD])
        wkvb_raw = sb("wkvb_raw", [R, NI, NI, NOPE])
        wo_g = sb("wo_g", [P, NI, C])
        xq_w = sb("xq_w", [P, C])
        xk_w = sb("xk_w", [P, C])
        xg_w = sb("xg_w", [P, C])
        gate_b = sb("gate_b", [1, C])
        normw_b = sb("normw_b", [P, C])
        ln1_w = sb("ln1_w", [P, 1])
        ln2_w = sb("ln2_w", [P, 1])
        gx = sb("gx", [P, 1])
        gf = sb("gf", [P, 1])
        ebias = sb("ebias", [P, NE])
        wgate_raw = sb("wgate_raw", [P, NE])
        wgu_raw = sb("wgu_raw", [P, 2 * NE + 2, EI])
        wd = sb("wd", [P, NP, C])
        swd = sb("swd", [EI, C])

        identb = sb("identb", [P, P], bf16)
        maskb = sb("maskb", [P, P], bf16)
        warm_in = sb("warm_in", [P, 512], bf16)
        ln1_s = sb("ln1_s", [P, 1])
        tgx = sb("tgx", [P, 1])
        tgf = sb("tgf", [P, 1])
        wqn = sb("wqn", [P, NI, NI, NOPE])
        wqnT = sb("wqnT", [P, NI, P])
        bd = sb("bd", [P, NI, NI * R])
        wn = sb("wn", [P, NH, R])
        wr = sb("wr", [P, NH, 2, HALF])
        ka = sb("ka", [P, KD])
        wvo = sb("wvo", [P, 2, C])
        aqk = sb("aqk", [P, C])
        xgT = sb("xgT", [P, C])
        wgate = sb("wgate", [P, NE])
        wgu = sb("wgu", [P, 2 * NE + 2, EI])
        wr2 = sb("wr2", [P, 2, NH * ROPE], f32r)
        wn2 = sb("wn2", [P, 2, NH * R], f32r)
        wgu2 = sb("wgu2", [P, 2, 2 * NE + 2, EI], f32r)
        gate_r1 = sb("gate_r1", [1, C])
        gate_r2 = sb("gate_r2", [1, C])
        gate_h = sb("gate_h", [1, 2, C], bf16)
        gate_b3 = sb("gate_b3", [2 * 32 + 1, NT, C], bf16)
        ones3 = sb("ones3", [2 * 32 + 1, P], bf16)

        x_all = sb("x_all", [P, B * NT, C])
        xi = sb("xi", [P, NT, C])
        cx = sb("cx", [P, NT, C])
        xo = sb("xo", [P, NT, C])
        h2_all = sb("h2_all", [P, B * NT, C])

        st = sb("st", [P, NT, 6])
        mv = sb("mv", [P, NT, 2])
        power = sb("power", [P, 3, NT])
        vv = sb("vv", [P, 3, NT])
        ss = sb("ss", [P, 3, NT])
        ratio = sb("ratio", [P, NT])
        tmp2 = sb("tmp2", [P, NT])
        hx = sb("hx", [P, NT, C])
        vx = sb("vx", [P, NT, C])
        poolT = sb("poolT", [P, 2 * S])
        hqT = sb("hqT", [P, 2, S])
        nmx = sb("nmx", [P, NT])
        rsx = sb("rsx", [P, NT])
        px = sb("px", [P, NT, 2 * S])
        pxT = sb("pxT", [P, 7, P])
        dx = sb("dx", [P, NT, C])
        thx = sb("thx", [P, NT, C])
        st2 = sb("st2", [P, NT, 6])
        mv2 = sb("mv2", [P, NT, 2])
        vv2 = sb("vv2", [P, 2, NT])
        ss2 = sb("ss2", [P, 2, NT])
        xn = sb("xn", [P, NT, C])
        xnT = sb("xnT", [P, S])
        xnT2 = sb("xnT2", [P, 2, S], f32r)

        latn = sb("latn", [P, NT, R])
        lat1 = sb("lat1", [P, NT, 2 * R])
        kf = sb("kf", [P, NT, KD])
        kt1 = sb("kt1", [P, NT, 2, HALF])
        kt2 = sb("kt2", [P, NT, 2, HALF])
        ks = sb("ks", [P, 2, NT, P], f32r)
        kTa = sb("kTa", [P, 2, NT, P], f32r)
        kTb = sb("kTb", [P, 2, NT, P], f32r)
        q1 = sb("q1", [P, NH, 2, HALF])
        q2 = sb("q2", [P, NH, 2, HALF])
        qf = sb("qf", [P, NH, KD])
        qs = sb("qs", [P, NH, 2, KD], f32r)
        qT = sb("qT", [P, NT, NH, P], f32r)
        mx = sb("mx", [P, NT, NH])
        mT = sb("mT", [NH, NT, P], f32r)
        pT = sb("pT", [P, 3, NI, 512])
        zs = sb("zs", [P, 512])
        rc = sb("rc", [P, NI, NI, 1])
        yn = sb("yn", [P, NI, NI, R])
        ynT = sb("ynT", [P, 2, P])

        sq = sb("sq", [P, NT, C])
        ms = sb("ms", [P, NT])
        r3 = sb("r3", [P, NT])
        x3 = sb("x3", [P, NT, C])
        xn3 = sb("xn3", [P, NT, C])
        n3T = sb("n3T", [P, S])
        n3T2 = sb("n3T2", [P, 2, S], f32r)
        logits = sb("logits", [P, NT, NE])
        best = sb("best", [P, NT, 8])
        besti = sb("besti", [P, NT, 8], mybir.dt.uint32)
        bestf = sb("bestf", [P, NT, 8])
        oh1 = sb("oh1", [P, NT, NE])
        oh2 = sb("oh2", [P, NT, NE])
        dm = sb("dm", [P, NT, 1])
        e2 = sb("e2", [P, NT, 1])
        p1 = sb("p1", [P, NT, 1])
        oh = sb("oh", [P, NT, NE])
        comb = sb("comb", [P, NT, NE])
        comb2 = sb("comb2", [P, NT, 2, NE], f32r)
        combT = sb("combT", [2 * NE, S], f32r)
        sel = sb("sel", [2 * NE, NP, P], f32r)
        th = sb("th", [P, NP + 1, S])
        s1 = sb("s1", [P, NP + 1, S])
        hid = sb("hid", [P, NP + 1, S])
        fin = sb("fin", [P, NT, C])
        outt = sb("outt", [P, NT, C])

        pA, pB, pV = pb("pA"), pb("pB"), pb("pV")
        wa, wb = pb("wa"), pb("wb")
        wf = pb("wf")
        wm = [pb("wm0"), pb("wm1")]

        names = """consts_in weights_in xw_in x_in c_in spread_in x_mixed x_kept ms_ready consts_ready warm_ready wqn_ready wqnT_psum wqnT_ready wkvbT_psum
            bd_ready absorb_psum xweights_psum weights_ready act_setup pool_setup xw_ready
            var1_ready scale1_ready vx_ready poolT_psum poolT_ready hqT_psum hqT_ready lx_psum nmx_ready px_ready
            pxT_psum pxT_ready z_psum thx_ready hx_psum var2_ready scale2_ready xn_ready xnT_psum xnT_ready xnT_low wr_ready wgu_ready wr2_high wn2_high wgu2_high wgu2_low split_ready gate_b3_ready n3T_low
            ckv_psum k_lat k_split ksT_psum kTa_ready kTb_ready lat1_ready
            q_psum q_rope q_nope q_full q_high q_low qT_psum qT_ready
            a_psum mx_ready mT_psum mT_ready minus_max_in b_psum exp_ready masked
            pv_psum zs_ready zsT_psum yn_ready ynT_psum ynT_ready y_psum x3_ready x3_copied var3_ready scale3_ready
            xn3_ready n3T_psum n3T_ready lg_psum dm_ready e2_ready comb_ready combT_psum combT_ready
            combB_psum gu_psum th_ready gu_read hid_ready moe_psum moe_read out_ready out_done
            chain_setup chain_front chain_keys chain_attn chain_experts dve_passed pool_passed""".split()
        s = {n: sem(n) for n in names}

        def wait(eng, name, value):
            if not (isinstance(value, int) and value <= 0):
                eng.wait_ge(s[name], value)

        class Chain:

            def __init__(self, eng, name, per, i):
                self.eng, self.name, self.per, self.i, self.n = eng, name, per, i, 0

            def __call__(self, ins):
                self.n += 1
                ins.then_inc(s[self.name], 1)
                self.eng.wait_ge(s[self.name], self.per * self.i + self.n)

        NW, NX = 16 * 20, 16 * 4
        NU = 12

        def unit(b, t, n):
            return NU * b + NI * t + n + 1

        def maxima_bank(t, u):
            return wm[0] if t == 1 and u % 2 else pA

        block = ctx.enter_context(nc.Block())

        def schedule(eng, round_):
            round_(-2)
            round_(-1)
            round_(0)
            with eng.Fori(1, B - 2) as i:
                round_(i)
            round_(B - 2)
            round_(B - 1)
            round_(B)

        def has(i):
            if not isinstance(i, int):
                return False, True, True, True, True
            return i == -2, i + 2 < B, 0 <= i + 1 < B, 0 <= i < B, i >= 1

        @block.sync
        def _(sp):
            def load(b):
                wait(sp, "x_mixed", b)
                sp.dma_start(xi[:], t_in["x"][bass.ds(b, 1), :, :].rearrange("b (t p) c -> p (b t) c", p=P)).then_inc(s["x_in"], 16)
                wait(sp, "hx_psum", b)
                sp.dma_start(cx[:], t_in["ctx_1024"][bass.ds(b, 1), :, :].rearrange("b (t p) c -> p (b t) c", p=P)).then_inc(s["c_in"], 16)

            load(0)
            sp.sem_inc(s["out_done"], 16)
            sp.dma_start(consts[:], t_in["c_consts"]).then_inc(s["consts_in"], 16)
            sp.dma_start(xg_w[:], t_in["L0_xattn_gate_w"]).then_inc(s["xw_in"], 16)
            sp.dma_start(gate_b[:], t_in["L0_xattn_gate_b"].rearrange("(a c) -> a c", a=1)).then_inc(s["xw_in"], 16)
            sp.dma_start(sel_f[:], t_in["c_sel"]).then_inc(s["weights_in"], 16)
            sp.dma_start(ln1_w[:], t_in["L0_ffn_w_ln1"].rearrange("(c a) -> c a", a=1)).then_inc(s["weights_in"], 16)
            sp.dma_start(ln2_w[:], t_in["L0_ffn_w_ln2"].rearrange("(c a) -> c a", a=1)).then_inc(s["weights_in"], 16)
            sp.dma_start(wq_raw[:], t_in["L0_ffn_Wq"].rearrange("c (h d) -> c h d", h=NH)).then_inc(s["weights_in"], 16)
            wkvb_v = t_in["L0_ffn_Wkvb"].rearrange("l (j i d) -> i l j d", j=NI, i=NI)
            for m in range(NI):
                sp.dma_start(wkvb_raw[:, m, :, :], wkvb_v[m]).then_inc(s["weights_in"], 16)
            sp.dma_start(wkva_raw[:], t_in["L0_ffn_Wkva"]).then_inc(s["weights_in"], 16)
            wo_v = t_in["L0_ffn_Wo"].rearrange("(j i e d) c -> j e d i c", j=NI, i=NI, e=2)
            for j in range(NI):
                sp.dma_start(wo_g[NOPE * j:NOPE * (j + 1), :, :], wo_v[j, 0]).then_inc(s["weights_in"], 16)
            sp.dma_start(wgate_raw[:], t_in["L0_ffn_Wgate"]).then_inc(s["weights_in"], 16)
            for n, (big, small) in enumerate([("L0_ffn_Wg", "L0_ffn_sWg"), ("L0_ffn_Wu", "L0_ffn_sWu")]):
                sp.dma_start(wgu_raw[:, NE * n:NE * (n + 1), :], t_in[big].rearrange("e c i -> c e i")).then_inc(s["weights_in"], 16)
                sp.dma_start(wgu_raw[:, 2 * NE + n, :], t_in[small][0]).then_inc(s["weights_in"], 16)
            sp.dma_start(wd[:], t_in["L0_ffn_Wd"].rearrange("(p e) i c -> (e i) p c", e=2)).then_inc(s["weights_in"], 16)
            sp.dma_start(swd[:], t_in["L0_ffn_sWd"][0]).then_inc(s["weights_in"], 16)

            def minus_max(b, t):
                sp.wait_ge(s["mT_ready"], NT * b + t + 1)
                sp.dma_start(qT[QROW:QROW + 1, t, :, :].bitcast(f32), mT[:, t, :].bitcast(f32)).then_inc(s["minus_max_in"], 16)

            def round_(i):
                setup, front, queries, weights, experts = has(i)
                if front and not setup:
                    load(i + 2)
                if weights:
                    minus_max(i, 1)
                if queries:
                    minus_max(i + 1, 0)
                if experts:
                    sp.wait_ge(s["out_ready"], i)
                    sp.dma_start(out_d[bass.ds(i - 1, 1), :, :].rearrange("b (t p) c -> p (b t) c", p=P), outt[:]).then_inc(s["out_done"], 16)

            schedule(sp, round_)
            sp.wait_ge(s["out_done"], 16 * (B + 1))

        @block.gpsimd
        def _(pool):
            pool.memset(power[:, 0:2, :], -0.5)
            for dst, src in [(normw_b[:], t_in["L0_xattn_norm_w"].partition_broadcast(P)),
                             (gx[:], t_in["g_xattn"].partition_broadcast(P)), (gf[:], t_in["g_ffn"].partition_broadcast(P)),
                             (ebias[:], t_in["L0_ffn_expert_bias"].partition_broadcast(P))]:
                pool.dma_start(dst, src).then_inc(s["spread_in"], 16)
            pool.memset(power[:, 2, :], 0.5).then_inc(s["pool_setup"], 1)
            pool.memset(bd[:], 0.0).then_inc(s["pool_setup"], 1)
            pool.memset(lat1[:], 1.0).then_inc(s["pool_setup"], 1)
            pool.wait_ge(s["pool_setup"], 3)

            def scale1(b):
                pool.wait_ge(s["var1_ready"], b + 1)
                pool.tensor_tensor(ss[:], vv[:], power[:], ALU.pow).then_inc(s["scale1_ready"], 1)

            def scale2(b):
                pool.wait_ge(s["var2_ready"], b + 1)
                pool.tensor_tensor(ss2[:], vv2[:], power[:, 0:2, :], ALU.pow).then_inc(s["scale2_ready"], 1)

            def scale3(b):
                pool.wait_ge(s["var3_ready"], b + 1)
                pool.tensor_tensor(r3[:], ms[:], power[:, 0, :], ALU.pow).then_inc(s["scale3_ready"], 1)

            def split_rope_weights():
                pool.wait_ge(s["wr2_high"], 1)
                pool.tensor_tensor(wr2[:, 1, :], wr[:].rearrange("p h e d -> p (h e d)"), wr2[:, 0, :].bitcast(f32), ALU.subtract).then_inc(s["split_ready"], 1)

            def split_nope_weights():
                pool.wait_ge(s["wn2_high"], 1)
                pool.tensor_tensor(wn2[:, 1, :], wn[:].rearrange("p h l -> p (h l)"), wn2[:, 0, :].bitcast(f32), ALU.subtract).then_inc(s["split_ready"], 1)

            def split_expert_weights():
                pool.wait_ge(s["wgu2_high"], 1)
                pool.tensor_tensor(wgu2[:, 1, :, :], wgu[:], wgu2[:, 0, :, :].bitcast(f32), ALU.subtract).then_inc(s["wgu2_low"], 1)

            def normed_low(b):
                pool.wait_ge(s["xnT_ready"], 2 * b + 2)
                pool.tensor_tensor(xnT2[:, 1, :], xnT[:], xnT2[:, 0, :].bitcast(f32), ALU.subtract).then_inc(s["xnT_low"], 1)

            def normed3_low(b):
                pool.wait_ge(s["n3T_ready"], 2 * b + 2)
                pool.tensor_tensor(n3T2[:, 1, :], n3T[:], n3T2[:, 0, :].bitcast(f32), ALU.subtract).then_inc(s["n3T_low"], 1)

            def rotated(b, t):
                pool.wait_ge(s["q_rope"], NT * b + t + 1)
                pool.tensor_tensor(qf[:, :, R:KD], q1[:].rearrange("p h e d -> p h (e d)"),
                                   q2[:].rearrange("p h e d -> p h (e d)"), ALU.add).then_inc(s["q_full"], 1)

            def low(b, t):
                pool.wait_ge(s["q_high"], NT * b + t + 1)
                pool.tensor_tensor(qs[:, :, 1, :], qf[:], qs[:, :, 0, :].bitcast(f32), ALU.subtract).then_inc(s["q_low"], 1)

            def mask(b, t, g):
                pool.wait_ge(s["exp_ready"], unit(b, t, NI * t + g))
                pool.sem_inc(s["pool_passed"], 1)
                pool.affine_select(out=pT[:, 2 * t, g, :], in_=pT[:, 2 * t, g, :], compare_op=ALU.is_ge, fill=0.0,
                                   base=0, pattern=[[0, NI], [1, P]], channel_multiplier=-1).then_inc(s["masked"], 1)

            def round_(i):
                setup, front, queries, weights, experts = has(i)
                if front:
                    scale1(i + 2)
                if weights:
                    mask(i, 0, 0)
                if setup:
                    split_rope_weights()
                if queries:
                    rotated(i + 1, 0)
                if weights:
                    mask(i, 0, 1)
                if queries:
                    low(i + 1, 0)
                if experts:
                    scale3(i - 1)
                if weights:
                    mask(i, 0, 2)
                    mask(i, 0, 3)
                if experts:
                    normed3_low(i - 1)
                if queries:
                    rotated(i + 1, 1)
                if setup:
                    split_nope_weights()
                    split_expert_weights()
                if queries:
                    low(i + 1, 1)
                if weights:
                    mask(i, 1, 0)
                    mask(i, 1, 1)
                if front:
                    scale2(i + 2)
                if weights:
                    mask(i, 1, 2)
                    mask(i, 1, 3)
                if front:
                    normed_low(i + 2)

            schedule(pool, round_)

        @block.scalar
        def _(act):
            act.dma_start(xq_w[:], t_in["L0_xattn_q_w"]).then_inc(s["xw_in"], 16)
            act.dma_start(xk_w[:], t_in["L0_xattn_k_w"]).then_inc(s["xw_in"], 16)

            def cross_weights():
                act.wait_ge(s["xweights_psum"], 1)
                act.activation(aqk[:], pV[:, 0:C], ACT.Copy, scale=C ** -0.5).then_inc(s["xw_ready"], 1)
                act.activation(xgT[:], pV[:, C:2 * C], ACT.Copy).then_inc(s["xw_ready"], 1)
                act.wait_ge(s["spread_in"], 16 * 4)
                act.activation(tgx[:], gx[:], ACT.Tanh).then_inc(s["xw_ready"], 1)
                act.activation(tgf[:], gf[:], ACT.Tanh).then_inc(s["xw_ready"], 1)

            def nope_weights():
                act.wait_ge(s["weights_in"], NW)
                act.activation(ln1_s[:], ln1_w[:], ACT.Copy, scale=DH ** -0.5).then_inc(s["act_setup"], 1)
                act.wait_ge(s["act_setup"], 1)
                act.activation(wqn[:], wq_raw[:, :, 0:NOPE].rearrange("p (j i) d -> p i j d", i=NI), ACT.Copy, scale=ln1_s[:, 0:1]).then_inc(s["wqn_ready"], 1)

            def rope_weights():
                act.activation(wr[:].rearrange("p h e d -> p h d e"), wq_raw[:, :, NOPE:DH].rearrange("p h (d e) -> p h d e", e=2), ACT.Copy, scale=ln1_s[:, 0:1]).then_inc(s["wr_ready"], 1)

            def key_weights():
                act.activation(ka[:, 0:R], wkva_raw[:, 0:R], ACT.Copy, scale=ln1_w[:, 0:1]).then_inc(s["act_setup"], 1)
                act.activation(ka[:, R:KD].rearrange("p (e d) -> p d e", e=2), wkva_raw[:, R:KD].rearrange("p (d e) -> p d e", e=2), ACT.Copy, scale=ln1_w[:, 0:1]).then_inc(s["act_setup"], 1)
                act.activation(wgate[:], wgate_raw[:], ACT.Copy, scale=ln2_w[:, 0:1]).then_inc(s["act_setup"], 1)

            def expert_weights():
                act.activation(wgu[:], wgu_raw[:], ACT.Copy, scale=ln2_w[:, 0:1]).then_inc(s["wgu_ready"], 1)

            def nope_weightsT():
                act.wait_ge(s["wqnT_psum"], 1)
                act.activation(wqnT[:], wa[:].rearrange("p (i c) -> p i c", i=NI), ACT.Copy).then_inc(s["wqnT_ready"], 1)

            def absorbed():
                act.wait_ge(s["absorb_psum"], 1)
                act.activation(wn[:].rearrange("p (j i) l -> p i j l", i=NI),
                               wb[:, 0:NH * R].rearrange("p (i j l) -> p i j l", i=NI, j=NI), ACT.Copy).then_inc(s["weights_ready"], 1)
                act.activation(wvo[:], wm[0][:, 0:2 * C].rearrange("p (a c) -> p a c", a=2), ACT.Copy).then_inc(s["weights_ready"], 1)

            def pool_tokens(b):
                act.wait_ge(s["poolT_psum"], b + 1)
                act.activation(poolT[:], wf[:], ACT.Copy).then_inc(s["poolT_ready"], 1)

            def x_queries(b):
                act.wait_ge(s["hqT_psum"], b + 1)
                act.activation(hqT[:], wf[:].rearrange("p (e s) -> p e s", e=2), ACT.Copy).then_inc(s["hqT_ready"], 1)

            def x_weights(b, t):
                act.wait_ge(s["nmx_ready"], NT * b + (1 - t) + 1)
                n = P * (t + 1) + S
                act.activation(px[:, t, 0:n], wf[:, 0:n], ACT.Exp, bias=nmx[:, t:t + 1], accum_out=rsx[:, t:t + 1]).then_inc(s["px_ready"], 1)

            def x_weightsT(b, t):
                act.wait_ge(s["pxT_psum"], NT * b + (1 - t) + 1)
                k0, n = (0, 4) if t == 1 else (4, 3)
                act.activation(pxT[:, k0:k0 + n, :], wf[:, 0:n * P].rearrange("p (k q) -> p k q", k=n), ACT.Copy).then_inc(s["pxT_ready"], 1)

            def x_gate(b):
                act.wait_ge(s["z_psum"], b + 1)
                act.activation(thx[:], wf[:, 0:S].rearrange("p (t c) -> p t c", t=NT), ACT.Tanh, scale=0.5).then_inc(s["thx_ready"], 1)

            def normed(b):
                act.wait_ge(s["xnT_psum"], b + 1)
                act.activation(xnT[:], wf[:, 0:S], ACT.Copy).then_inc(s["xnT_ready"], 1)
                act.activation(xnT2[:, 0, :], wf[:, 0:S], ACT.Copy).then_inc(s["xnT_ready"], 1)

            def keep_x(b):
                act.wait_ge(s["x_mixed"], b + 1)
                act.activation(x_all[:, bass.ds(NT * b, NT), :], xo[:], ACT.Copy).then_inc(s["x_kept"], 1)

            def latent(b):
                wait(act, "lat1_ready", b)
                act.wait_ge(s["ckv_psum"], b + 1)
                ckv = wm[1][:, 0:NT * KD].rearrange("p (t d) -> p t d", t=NT)
                act.activation(latn[:], ckv[:, :, 0:R], ACT.Copy).then_inc(s["k_lat"], 1)
                act.activation(kf[:, :, 0:R], ckv[:, :, 0:R], ACT.Copy).then_inc(s["k_lat"], 1)

            def keys(b):
                act.wait_ge(s["ksT_psum"], b + 1)
                act.activation(kTa[:], pV[:].rearrange("p (e t q) -> p e t q", e=2, t=NT), ACT.Copy).then_inc(s["kTa_ready"], 1)

            def nope(b, t):
                act.wait_ge(s["q_psum"], NT * b + t + 1)
                act.activation(qf[:, :, 0:R], wb[:, 0:NH * R].rearrange("p (h l) -> p h l", h=NH), ACT.Copy).then_inc(s["q_nope"], 1)

            def high(b, t):
                act.wait_ge(s["q_full"], NT * b + t + 1)
                act.wait_ge(s["q_nope"], NT * b + t + 1)
                act.activation(qs[:, :, 0, :], qf[:], ACT.Copy).then_inc(s["q_high"], 1)

            def queriesT(b, t, g):
                act.wait_ge(s["qT_psum"], NI * (NT * b + t) + g + 1)
                act.activation(qT[0:QROW, t, NI * g:NI * (g + 1), :], [wa, wb][g % 2][0:QROW, :].rearrange("p (h q) -> p h q", h=NI), ACT.Copy).then_inc(s["qT_ready"], 1)

            def minus_max(b, t):
                act.wait_ge(s["mT_psum"], NT * b + t + 1)
                act.activation(mT[:, t, :], pA[0:NH, 0:P], ACT.Copy, scale=-1.0).then_inc(s["mT_ready"], 1)

            def weights_(b, t, kt, g):
                act.wait_ge(s["b_psum"], unit(b, t, NI * kt + g))
                act.activation(pT[:, t + kt, g, :], pB[:], ACT.Exp).then_inc(s["exp_ready"], 1)

            def values(b, t):
                act.wait_ge(s["pv_psum"], NT * b + t + 1)
                act.activation(zs[:], pV[:], ACT.Copy).then_inc(s["zs_ready"], 1)

            def valuesT(b, t):
                act.wait_ge(s["ynT_psum"], NT * b + t + 1)
                act.activation(ynT[:], pV[:, 0:2 * P].rearrange("p (a q) -> p a q", a=2), ACT.Copy).then_inc(s["ynT_ready"], 1)

            def squares(b):
                act.wait_ge(s["x3_copied"], b + 1)
                for t in range(NT):
                    act.activation(sq[:, t, :], x3[:, t, :], ACT.Square, accum_out=ms[:, t:t + 1]).then_inc(s["ms_ready"], 1)

            def normed3(b):
                act.wait_ge(s["n3T_psum"], b + 1)
                act.activation(n3T[:], wm[0][:, 0:S], ACT.Copy).then_inc(s["n3T_ready"], 1)
                act.activation(n3T2[:, 0, :], wm[0][:, 0:S], ACT.Copy).then_inc(s["n3T_ready"], 1)

            def second_best(b):
                act.wait_ge(s["dm_ready"], b + 1)
                act.activation(e2[:], dm[:], ACT.Exp).then_inc(s["e2_ready"], 1)

            def combT_(b):
                act.wait_ge(s["combT_psum"], b + 1)
                act.activation(combT[:], wm[0][0:2 * NE, 0:S], ACT.Copy).then_inc(s["combT_ready"], 1)

            def gate(b, p):
                rows = P if p < NP else EI
                act.wait_ge(s["gu_psum"], (NP + 1) * b + p + 1)
                act.activation(th[0:rows, p, :], wm[(p + 1) % 2][0:rows, 0:S], ACT.Tanh, scale=0.5).then_inc(s["th_ready"], 1)

            def round_(i):
                setup, front, queries, weights, experts = has(i)
                if setup:
                    cross_weights()
                if experts:
                    values(i - 1, 1)
                if weights:
                    weights_(i, 0, 0, 0)
                if front:
                    pool_tokens(i + 2)
                if queries:
                    latent(i + 1)
                if experts:
                    valuesT(i - 1, 1)
                if queries:
                    nope(i + 1, 0)
                if weights:
                    weights_(i, 0, 0, 1)
                if front:
                    x_queries(i + 2)
                if queries:
                    high(i + 1, 0)
                if weights:
                    weights_(i, 0, 0, 2)
                if setup:
                    nope_weights()
                if experts:
                    squares(i - 1)
                if front:
                    x_weights(i + 2, 1)
                if weights:
                    weights_(i, 0, 0, 3)
                if queries:
                    keys(i + 1)
                if weights:
                    minus_max(i, 1)
                if experts:
                    normed3(i - 1)
                if queries:
                    queriesT(i + 1, 0, 0)
                    queriesT(i + 1, 0, 1)
                if setup:
                    nope_weightsT()
                if front:
                    x_weights(i + 2, 0)
                if experts:
                    gate(i - 1, 0)
                if queries:
                    queriesT(i + 1, 0, 2)
                if weights:
                    values(i, 0)
                if experts:
                    second_best(i - 1)
                if weights:
                    weights_(i, 1, 0, 0)
                if experts:
                    gate(i - 1, 1)
                    gate(i - 1, 2)
                if queries:
                    queriesT(i + 1, 0, 3)
                if front:
                    x_weightsT(i + 2, 1)
                if setup:
                    absorbed()
                if weights:
                    weights_(i, 1, 0, 1)
                if experts:
                    gate(i - 1, 3)
                if front:
                    x_weightsT(i + 2, 0)
                if weights:
                    weights_(i, 1, 0, 2)
                if experts:
                    gate(i - 1, 4)
                if weights:
                    weights_(i, 1, 0, 3)
                if setup:
                    rope_weights()
                    key_weights()
                if front:
                    x_gate(i + 2)
                if experts:
                    combT_(i - 1)
                if setup:
                    expert_weights()
                if queries:
                    nope(i + 1, 1)
                if weights:
                    weights_(i, 1, 1, 0)
                if queries:
                    high(i + 1, 1)
                if weights:
                    weights_(i, 1, 1, 1)
                    valuesT(i, 0)
                    weights_(i, 1, 1, 2)
                if queries:
                    minus_max(i + 1, 0)
                    queriesT(i + 1, 1, 0)
                    queriesT(i + 1, 1, 1)
                if weights:
                    weights_(i, 1, 1, 3)
                if front:
                    keep_x(i + 2)
                if queries:
                    queriesT(i + 1, 1, 2)
                    queriesT(i + 1, 1, 3)
                if front:
                    normed(i + 2)

            schedule(act, round_)

        @block.tensor
        def _(pe):
            def mm(out, lhsT, rhs, start=True, stop=True):
                return pe.matmul(out, lhsT, rhs, start=start, stop=stop)

            def cross_weights():
                pe.wait_ge(s["consts_in"], 16)
                pe.wait_ge(s["xw_in"], NX)
                mm(pV[:, 0:C], xq_w[:], xk_w[:])
                pe.transpose(pV[:, C:2 * C], xg_w[:], ident).then_inc(s["xweights_psum"], 1)
                pe.wait_ge(s["consts_ready"], 1)
                pe.wait_ge(s["pool_setup"], 3)

            def value_weightsT():
                pe.wait_ge(s["weights_in"], NW)
                for m in range(NI):
                    last = pe.transpose(wb[:, R * m:R * (m + 1)], wkvb_raw[:, m, :, :].rearrange("l j d -> l (j d)"), ident[0:R, 0:R])
                last.then_inc(s["wkvbT_psum"], 1)

            def nope_weightsT():
                pe.wait_ge(s["wqn_ready"], 1)
                for m in range(NI):
                    last = pe.transpose(wa[:, P * m:P * (m + 1)], wqn[:, m, :, :].rearrange("p j d -> p (j d)"), ident)
                last.then_inc(s["wqnT_psum"], 1)

            def absorbed():
                pe.wait_ge(s["bd_ready"], 1)
                pe.wait_ge(s["wqnT_ready"], 1)
                for m in range(NI):
                    mm(wb[:, NI * R * m:NI * R * (m + 1)], wqnT[:, m, :], bd[:, m, :])
                    half = slice(EI * (m % 2), EI * (m % 2 + 1))
                    last = mm(wm[0][half, C * (m // 2):C * (m // 2 + 1)], bd[:, m, :], wo_g[:, m, :])
                last.then_inc(s["absorb_psum"], 1)

            def weights_made():
                pe.wait_ge(s["act_setup"], 4)
                pe.wait_ge(s["weights_ready"], 2)
                pe.wait_ge(s["split_ready"], 2)

            def keep_warm(i, n):
                pe.wait_ge(s["warm_ready"], 1)
                if i == B:
                    pe.wait_ge(s["exp_ready"], NU * B)
                for _ in range(n):
                    mm(pB[:], warm_in[:, 0:P], warm_in[:])

            def pool_tokens(b):
                pe.wait_ge(s["vx_ready"], b + 1)
                pe.wait_ge(s["c_in"], 16 * (b + 1))
                wait(pe, "xnT_ready", 2 * b)
                for t in range(NT):
                    pe.transpose(wf[:, P * t:P * (t + 1)], vx[:, t, :], ident)
                    last = pe.transpose(wf[:, S + P * t:S + P * (t + 1)], cx[:, t, :], ident)
                last.then_inc(s["poolT_psum"], 1)

            def x_queries(b):
                pe.wait_ge(s["poolT_ready"], b + 1)
                pe.wait_ge(s["xw_ready"], 2)
                for t in range(NT):
                    pe.transpose(wf[:, P * t:P * (t + 1)], hx[:, t, :], ident)
                mm(wf[:, S:2 * S], aqk[:], poolT[:, 0:S]).then_inc(s["hqT_psum"], 1)

            def x_scores(b, t):
                if t == 1:
                    pe.wait_ge(s["hqT_ready"], b + 1)
                    mm(wf[:], hqT[:, 1, P:2 * P], poolT[:], stop=False)
                    mm(wf[:, P:2 * P], identb[:], maskb[:], start=False).then_inc(s["lx_psum"], 1)
                else:
                    pe.wait_ge(s["px_ready"], NT * b + 1)
                    mm(wf[:, 0:P], hqT[:, 1, 0:P], poolT[:, 0:P], stop=False)
                    mm(wf[:, 0:P], identb[:], maskb[:], start=False)
                    mm(wf[:, P:P + S], hqT[:, 1, 0:P], poolT[:, S:2 * S]).then_inc(s["lx_psum"], 1)

            def x_weightsT(b, t):
                pe.wait_ge(s["px_ready"], NT * b + NT)
                if t == 0:
                    pe.wait_ge(s["pxT_ready"], NT * b + 1)
                for k in range(3 + t):
                    last = pe.transpose(wf[:, P * k:P * (k + 1)], px[:, t, P * k:P * (k + 1)], ident)
                last.then_inc(s["pxT_psum"], 1)

            def x_gate(b):
                pe.wait_ge(s["pxT_ready"], NT * b + NT)
                if isinstance(b, int) and b == 0:
                    pe.wait_ge(s["gate_b3_ready"], 1)
                for t in range(NT):
                    mm(wf[:, P * t:P * (t + 1)], hqT[:, 0, P * t:P * (t + 1)], xgT[:], start=t == 0, stop=False)
                mm(wf[:, 0:NT * C], ones3[:], gate_b3[:].rearrange("p t c -> p (t c)"), start=False).then_inc(s["z_psum"], 1)

            def x_values(b):
                pe.wait_ge(s["thx_ready"], b + 1)
                vals = [vx[:, 0, :], vx[:, 1, :], cx[:, 0, :], cx[:, 1, :]]
                for k, v in enumerate([vals[0], vals[2], vals[3]]):
                    mm(wf[:, 0:P], pxT[:, 4 + k, :], v, start=k == 0, stop=k == 2)
                for k, v in enumerate(vals):
                    last = mm(wf[:, P:2 * P], pxT[:, k, :], v, start=k == 0, stop=k == 3)
                last.then_inc(s["hx_psum"], 1)

            def normed(b):
                pe.wait_ge(s["xn_ready"], b + 1)
                for t in range(NT):
                    last = pe.transpose(wf[:, P * t:P * (t + 1)], xn[:, t, :], ident)
                last.then_inc(s["xnT_psum"], 1)

            def queries_(b, t):
                if t == 0:
                    pe.wait_ge(s["xnT_low"], b + 1)
                wait(pe, "qT_ready", NI * (NT * b + t))
                parts = [(1, 0), (0, 0), (0, 1)]
                for n, (e, w) in enumerate(parts):
                    q = xnT2[:, e, P * t:P * (t + 1)]
                    mm(wa[:], q, wr2[:, w, :], start=n == 0, stop=n == 2)
                    last = mm(wb[:, 0:NH * R], q, wn2[:, w, :], start=n == 0, stop=n == 2)
                last.then_inc(s["q_psum"], 1)

            def queriesT(b, t, g):
                if g == 0:
                    pe.wait_ge(s["q_low"], NT * b + t + 1)
                if g >= 2:
                    pe.wait_ge(s["qT_ready"], NI * (NT * b + t) + g - 1)
                for h in range(NI):
                    last = pe.transpose([wa, wb][g % 2][0:QROW, P * h:P * (h + 1)], qs[:, NI * g + h, :, :].bitcast(f32).rearrange("p e d -> p (e d)"), ident)
                last.then_inc(s["qT_psum"], 1)

            def latent(b):
                pe.wait_ge(s["xnT_ready"], 2 * b + 1)
                wait(pe, "moe_read", b - 1)
                for t in range(NT):
                    last = mm(wm[1][:, KD * t:KD * (t + 1)], xnT[:, P * t:P * (t + 1)], ka[:])
                last.then_inc(s["ckv_psum"], 1)

            def keys(b):
                pe.wait_ge(s["k_split"], b + 1)
                wait(pe, "x3_ready", NT * (b - 1))
                for e in range(2):
                    for t in range(NT):
                        last = pe.transpose(pV[:, (NT * e + t) * P:(NT * e + t + 1) * P], ks[:, e, t, :].bitcast(f32), ident)
                last.then_inc(s["ksT_psum"], 1)

            def maxima(b, t, u):
                nk = P * (t + 1)
                per = 512 // nk
                if t == 0 and u == 0:
                    pe.wait_ge(s["kTa_ready"], b + 1)
                if u == 0:
                    wait(pe, "mT_ready", NT * b + t)
                if per * u % NI == 0:
                    pe.wait_ge(s["qT_ready"], NI * (NT * b + t) + (per * u) // NI + 1)
                wait(pe, "mx_ready", unit(b, t, u) - (2 if t == 1 and u > 0 else 1))
                if t == 1 and u == 1:
                    wait(pe, "moe_read", b)
                pS = maxima_bank(t, u)
                for h in range(per):
                    mm(pS[:, nk * h:nk * (h + 1)], qT[0:QROW, t, per * u + h, :],
                       kTa[0:QROW, 0, 0:t + 1, :].rearrange("p t q -> p (t q)"), start=h == 0, stop=False)
                mm(pS[:].rearrange("p (h k) -> p h k", h=per)[:, :, P * t:P * (t + 1)], identb[:],
                   maskb[:].unsqueeze(1).to_broadcast([P, per, P]), start=False).then_inc(s["a_psum"], 1)

            def minus_max(b, t):
                pe.wait_ge(s["mx_ready"], unit(b, t, NI * (t + 1) - 1))
                pe.transpose(pA[0:NH, 0:P], mx[:, t, :], ident).then_inc(s["mT_psum"], 1)

            def weights_(b, t, kt, g):
                if kt == 0 and g == 0:
                    pe.wait_ge(s["minus_max_in"], 16 * (NT * b + t + 1))
                    if t == 0:
                        pe.wait_ge(s["kTb_ready"], b + 1)
                wait(pe, "exp_ready", unit(b, t, NI * kt + g) - 1)
                q = qT[0:QROW + 1, t, NI * g:NI * (g + 1), :].rearrange("p h q -> p (h q)")
                mm(pB[:], kTb[0:QROW + 1, 0, kt, :], q, stop=False)
                mm(pB[:], kTb[0:QROW + 1, 1, kt, :], q, start=False).then_inc(s["b_psum"], 1)

            def values(b, t):
                if t == 0:
                    pe.wait_ge(s["lat1_ready"], b + 1)
                    pe.wait_ge(s["kTa_ready"], min(b + 2, B) if isinstance(b, int) else b + 2)
                wait(pe, "x3_ready", NT * b + t)
                pe.wait_ge(s["masked"], NI * (NT * b + t + 1))
                for kt in range(t + 1):
                    for g in range(NI):
                        last = mm(pV[32 * g:32 * (g + 1), :], lat1[:, kt, :], pT[:, t + kt, g, :], start=kt == 0, stop=kt == t)
                last.then_inc(s["pv_psum"], 1)

            def values_by_query(b, t):
                pe.wait_ge(s["zs_ready"], NT * b + t + 1)
                for m in range(NI):
                    last = pe.transpose(pV[:, P * m:P * (m + 1)], zs[:, P * m:P * (m + 1)], ident)
                last.then_inc(s["zsT_psum"], 1)

            def valuesT(b, t):
                pe.wait_ge(s["yn_ready"], NT * b + t + 1)
                y = yn[:].rearrange("p m j l -> p (m j l)")
                for a in range(2):
                    last = pe.transpose(pV[:, P * a:P * (a + 1)], y[:, P * a:P * (a + 1)], ident)
                last.then_inc(s["ynT_psum"], 1)

            def project(b, t):
                pe.wait_ge(s["ynT_ready"], NT * b + t + 1)
                for a in range(2):
                    last = mm(pV[:, 0:C], ynT[:, a, :], wvo[:, a, :], start=a == 0, stop=a == 1)
                last.then_inc(s["y_psum"], 1)

            def normed3(b):
                pe.wait_ge(s["xn3_ready"], b + 1)
                pe.wait_ge(s["mx_ready"], min(unit(b + 1, 1, 2 * NI - 1), NU * B) if isinstance(b, int) else unit(b + 1, 1, 2 * NI - 1))
                for t in range(NT):
                    last = pe.transpose(wm[0][:, P * t:P * (t + 1)], xn3[:, t, :], ident)
                last.then_inc(s["n3T_psum"], 1)

            def router(b):
                pe.wait_ge(s["n3T_ready"], 2 * b + 2)
                for t in range(NT):
                    last = mm(wm[0][:, NE * t:NE * (t + 1)], n3T[:, P * t:P * (t + 1)], wgate[:])
                last.then_inc(s["lg_psum"], 1)

            def gate_up(b, p):
                w = wm[(p + 1) % 2]
                if p == 0:
                    pe.wait_ge(s["n3T_low"], b + 1)
                    if isinstance(b, int) and b == 0:
                        pe.wait_ge(s["wgu2_low"], 1)
                    pe.wait_ge(s["k_split"], min(b + 3, B) if isinstance(b, int) else b + 3)
                if p == 1:
                    pe.wait_ge(s["dm_ready"], b + 1)
                if p >= 2:
                    pe.wait_ge(s["gu_read"], (NP + 1) * b + p - 1)
                firsts = [2 * p, NE + 2 * p] if p < NP else [2 * NE]
                for m, first in enumerate(firsts):
                    for n, (e, part) in enumerate([(0, 0), (1, 0), (0, 1)]):
                        last = mm(w[:, S * m:S * (m + 1)], wgu2[:, part, first:first + 2, :].rearrange("p e i -> p (e i)"), n3T2[:, e, :], start=n == 0, stop=n == 2)
                last.then_inc(s["gu_psum"], 1)

            def combT_(b):
                pe.wait_ge(s["comb_ready"], b + 1)
                pe.wait_ge(s["gu_read"], (NP + 1) * b + NP)
                for t in range(NT):
                    last = pe.transpose(wm[0][0:2 * NE, P * t:P * (t + 1)], comb2[:, t, :, :].bitcast(f32).rearrange("p e n -> p (e n)"), ident)
                last.then_inc(s["combT_psum"], 1)

            def spread(b):
                pe.wait_ge(s["combT_ready"], b + 1)
                pe.wait_ge(s["gu_read"], (NP + 1) * (b + 1))
                for q in range(NP):
                    last = mm(wm[q // 2][:, S * (q % 2):S * (q % 2 + 1)], sel[:, q, :], combT[:])
                    if q % 2:
                        last.then_inc(s["combB_psum"], 1)

            def down(b):
                pe.wait_ge(s["hid_ready"], 2 * (b + 1))
                w = wm[0]
                for t in range(NT):
                    for p in range(NP):
                        mm(w[:, P * t:P * (t + 1)], hid[:, p, P * t:P * (t + 1)], wd[:, p, :], start=p == 0, stop=False)
                    last = mm(w[:, P * t:P * (t + 1)], hid[0:EI, NP, P * t:P * (t + 1)], swd[:], start=False)
                last.then_inc(s["moe_psum"], 1)

            def round_(i):
                setup, front, queries, weights, experts = has(i)
                if setup:
                    keep_warm(i, 23)
                    cross_weights()
                if weights:
                    maxima(i, 1, 0)
                    maxima(i, 1, 1)
                if experts and not weights:
                    keep_warm(i, 5)
                if experts:
                    values(i - 1, 1)
                if weights:
                    maxima(i, 1, 2)
                    maxima(i, 1, 3)
                    weights_(i, 0, 0, 0)
                if experts and not weights:
                    keep_warm(i, 3)
                if experts:
                    values_by_query(i - 1, 1)
                if queries and not weights:
                    keep_warm(i, 5)
                if queries:
                    queries_(i + 1, 0)
                if front and not weights:
                    keep_warm(i, 6)
                if setup:
                    keep_warm(i, 4)
                if front:
                    pool_tokens(i + 2)
                if weights:
                    maxima(i, 1, 4)
                if queries:
                    latent(i + 1)
                if experts and not weights:
                    keep_warm(i, 3)
                if experts:
                    valuesT(i - 1, 1)
                if weights:
                    weights_(i, 0, 0, 1)
                if front and not weights:
                    keep_warm(i, 3)
                if front:
                    x_queries(i + 2)
                if experts and not weights:
                    keep_warm(i, 2)
                if experts:
                    project(i - 1, 1)
                if weights:
                    weights_(i, 0, 0, 2)
                    maxima(i, 1, 5)
                if front and not weights:
                    keep_warm(i, 3)
                if front:
                    x_scores(i + 2, 1)
                if weights:
                    maxima(i, 1, 6)
                    weights_(i, 0, 0, 3)
                    maxima(i, 1, 7)
                if queries:
                    keys(i + 1)
                if setup:
                    keep_warm(i, 6)
                    value_weightsT()
                    keep_warm(i, 3)
                    nope_weightsT()
                if queries and not weights:
                    keep_warm(i, 4)
                if queries:
                    queriesT(i + 1, 0, 0)
                if front:
                    x_scores(i + 2, 0)
                if weights:
                    minus_max(i, 1)
                if setup:
                    keep_warm(i, 1)
                    absorbed()
                if experts and not weights:
                    keep_warm(i, 11)
                if experts:
                    normed3(i - 1)
                if queries:
                    queriesT(i + 1, 0, 1)
                if weights:
                    values(i, 0)
                if experts and not weights:
                    keep_warm(i, 3)
                if experts:
                    router(i - 1)
                if queries:
                    queriesT(i + 1, 0, 2)
                if experts and not weights:
                    keep_warm(i, 2)
                if experts:
                    gate_up(i - 1, 0)
                if queries:
                    maxima(i + 1, 0, 0)
                if weights:
                    weights_(i, 1, 0, 0)
                if experts:
                    gate_up(i - 1, 1)
                if experts and not weights:
                    keep_warm(i, 3)
                if experts:
                    gate_up(i - 1, 2)
                if queries:
                    queriesT(i + 1, 0, 3)
                if front:
                    x_weightsT(i + 2, 1)
                if weights:
                    weights_(i, 1, 0, 1)
                if experts and not weights:
                    keep_warm(i, 2)
                if experts:
                    gate_up(i - 1, 3)
                if queries:
                    maxima(i + 1, 0, 1)
                if front and not weights:
                    keep_warm(i, 1)
                if setup:
                    keep_warm(i, 2)
                if front:
                    x_weightsT(i + 2, 0)
                if weights:
                    weights_(i, 1, 0, 2)
                if experts and not weights:
                    keep_warm(i, 1)
                if experts:
                    gate_up(i - 1, 4)
                if weights:
                    values_by_query(i, 0)
                if queries:
                    queries_(i + 1, 1)
                if weights:
                    weights_(i, 1, 0, 3)
                if setup:
                    keep_warm(i, 3)
                if front:
                    x_gate(i + 2)
                if experts and not weights:
                    keep_warm(i, 5)
                if experts:
                    combT_(i - 1)
                if queries:
                    maxima(i + 1, 0, 2)
                if weights:
                    weights_(i, 1, 1, 0)
                if experts and not weights:
                    keep_warm(i, 2)
                if experts:
                    spread(i - 1)
                if front and not weights:
                    keep_warm(i, 1)
                if setup:
                    keep_warm(i, 1)
                if front:
                    x_values(i + 2)
                if weights:
                    valuesT(i, 0)
                    weights_(i, 1, 1, 1)
                if queries:
                    maxima(i + 1, 0, 3)
                if setup:
                    weights_made()
                if experts and not weights:
                    keep_warm(i, 4)
                if experts:
                    down(i - 1)
                if weights:
                    weights_(i, 1, 1, 2)
                if queries and not weights:
                    keep_warm(i, 8)
                if queries:
                    queriesT(i + 1, 1, 0)
                    minus_max(i + 1, 0)
                    queriesT(i + 1, 1, 1)
                if weights:
                    project(i, 0)
                    weights_(i, 1, 1, 3)
                if queries and not weights:
                    keep_warm(i, 2)
                if queries:
                    queriesT(i + 1, 1, 2)
                    queriesT(i + 1, 1, 3)
                if front and not weights:
                    keep_warm(i, 1)
                if setup:
                    keep_warm(i, 17)
                if front:
                    normed(i + 2)

            schedule(pe, round_)

        @block.vector
        def _(dve):
            V = nc.vector
            V.memset(warm_in[:], 0.0).then_inc(s["warm_ready"], 1)
            dve.sem_inc(s["moe_read"], 1)
            V.memset(ks[:].bitcast(f32), 0.0).then_inc(s["chain_setup"], 1)
            dve.wait_ge(s["chain_setup"], 1)
            V.memset(ks[:, 0, :, QROW:QROW + 1].bitcast(f32), 1.0)
            dve.wait_ge(s["consts_in"], 16)
            V.memset(gate_b3[:], 0.0)
            V.memset(ones3[:], 1.0)
            V.tensor_copy(identb[:], ident)
            V.tensor_copy(maskb[:], mask_f).then_inc(s["consts_ready"], 1)

            def gate_bias():
                link = Chain(dve, "chain_setup", 1, 1)
                dve.wait_ge(s["xw_in"], NX)
                link(V.tensor_copy(gate_h[:, 0, :], gate_b[:]))
                link(V.tensor_tensor(gate_r1[:], gate_b[:], gate_h[:, 0, :], ALU.subtract))
                link(V.tensor_copy(gate_h[:, 1, :], gate_r1[:]))
                link(V.tensor_tensor(gate_r2[:], gate_r1[:], gate_h[:, 1, :], ALU.subtract))
                for n, part in enumerate([gate_b, gate_r1, gate_r2]):
                    last = V.tensor_copy(gate_b3[32 * n:32 * n + 1, :, :], part[:].unsqueeze(1).to_broadcast([1, NT, C]))
                last.then_inc(s["gate_b3_ready"], 1)

            def split_rope_weights():
                dve.wait_ge(s["wr_ready"], 1)
                V.tensor_copy(wr2[:, 0, :], wr[:].rearrange("p h e d -> p (h e d)")).then_inc(s["wr2_high"], 1)

            def split_nope_weights():
                dve.wait_ge(s["weights_ready"], 1)
                V.tensor_copy(wn2[:, 0, :], wn[:].rearrange("p h l -> p (h l)")).then_inc(s["wn2_high"], 1)

            def split_expert_weights():
                dve.wait_ge(s["wgu_ready"], 1)
                V.tensor_copy(wgu2[:, 0, :, :], wgu[:]).then_inc(s["wgu2_high"], 1)

            def value_blocks():
                dve.wait_ge(s["pool_setup"], 3)
                dve.wait_ge(s["wkvbT_psum"], 1)
                V.tensor_copy(sel[:], sel_f[:])
                for j in range(NI):
                    rows = slice(NOPE * j, NOPE * (j + 1))
                    last = V.tensor_copy(bd[rows, :, R * j:R * (j + 1)], wb[rows, 0:NI * R].rearrange("p (i l) -> p i l", i=NI))
                last.then_inc(s["bd_ready"], 1)

            def flat(ap):
                return ap.rearrange("p t c -> p (t c)")

            def tiles(b):
                return bass.ds(NT * b, NT)

            def one(b, t):
                return bass.ds(NT * b + t, 1)

            front_chain, PER_FRONT = {}, 13
            expert_chain, PER_EXPERTS = {}, 14

            def norms(b):
                link = front_chain[0] = Chain(dve, "chain_front", PER_FRONT, b)
                dve.wait_ge(s["x_in"], 16 * (b + 1))
                for t in range(NT):
                    ins = V.bn_stats(st[:, t, :], xi[:, t, :])
                link(ins)
                for t in range(NT):
                    dve.sem_inc(s["dve_passed"], 1)
                    ins = V.bn_aggr(mv[:, t, :], st[:, t, :])
                link(ins)
                V.tensor_scalar(vv[:, 0, :], mv[:, :, 1], 1e-5, None, ALU.add)
                V.tensor_scalar(vv[:, 1, :], mv[:, :, 1], 1.0 + 1e-6, 1e-6 * 1e-5, ALU.mult, ALU.add)
                V.tensor_scalar(vv[:, 2, :], mv[:, :, 1], 1e-5, None, ALU.add).then_inc(s["var1_ready"], 1)

            def scaled(b):
                link = front_chain[0]
                dve.wait_ge(s["scale1_ready"], b + 1)
                if isinstance(b, int) and b == 0:
                    dve.wait_ge(s["spread_in"], 16 * 4)
                V.tensor_tensor(ratio[:], ss[:, 1, :], ss[:, 2, :], ALU.mult)
                for t in range(NT):
                    ins = V.tensor_scalar(hx[:, t, :], xi[:, t, :], mv[:, t, 0:1], ss[:, 0, t:t + 1], ALU.subtract, ALU.mult)
                link(ins)
                for t in range(NT):
                    ins = V.scalar_tensor_tensor(out=vx[:, t, :], in0=hx[:, t, :], scalar=ratio[:, t:t + 1], in1=normw_b[:], op0=ALU.mult, op1=ALU.mult)
                ins.then_inc(s["vx_ready"], 1)

            def x_max(b, t):
                link = front_chain[0]
                dve.wait_ge(s["lx_psum"], NT * b + (1 - t) + 1)
                n = P * (t + 1) + S
                link(V.tensor_reduce(tmp2[:, t:t + 1], wf[:, 0:n], op=ALU.max, axis=AX.X))
                V.tensor_scalar(nmx[:, t:t + 1], tmp2[:, t:t + 1], -1.0, None, ALU.mult).then_inc(s["nmx_ready"], 1)

            def mix(b):
                link = front_chain[0]
                dve.wait_ge(s["px_ready"], NT * (b + 1))
                link(V.reciprocal(tmp2[:], rsx[:]))
                dve.wait_ge(s["hx_psum"], b + 1)
                for t in range(NT):
                    ins = V.scalar_tensor_tensor(out=dx[:, t, :], in0=wf[:, P * t:P * (t + 1)], scalar=tmp2[:, t:t + 1], in1=hx[:, t, :], op0=ALU.mult, op1=ALU.subtract)
                link(ins)
                link(V.scalar_tensor_tensor(out=flat(dx[:]), in0=flat(thx[:]), scalar=1.0, in1=flat(dx[:]), op0=ALU.add, op1=ALU.mult))
                link(V.scalar_tensor_tensor(out=flat(dx[:]), in0=flat(dx[:]), scalar=0.5, in1=flat(hx[:]), op0=ALU.mult, op1=ALU.add))
                wait(dve, "x_kept", b)
                if isinstance(b, int) and b == 0:
                    dve.wait_ge(s["xw_ready"], 4)
                link(V.scalar_tensor_tensor(out=flat(xo[:]), in0=flat(dx[:]), scalar=tgx[:, 0:1], in1=flat(xi[:]), op0=ALU.mult, op1=ALU.add))
                dve.sem_inc(s["x_mixed"], 1)

            def norms2(b):
                link = front_chain[0]
                for t in range(NT):
                    ins = V.bn_stats(st2[:, t, :], xo[:, t, :])
                link(ins)
                for t in range(NT):
                    dve.sem_inc(s["dve_passed"], 1)
                    ins = V.bn_aggr(mv2[:, t, :], st2[:, t, :])
                link(ins)
                V.tensor_scalar(vv2[:, 0, :], mv2[:, :, 1], 1e-5, None, ALU.add)
                V.tensor_scalar(vv2[:, 1, :], mv2[:, :, 1], 1.0 + 1e-5, 1e-5 * 1e-5, ALU.mult, ALU.add).then_inc(s["var2_ready"], 1)

            def normed(b):
                link = front_chain[0]
                dve.wait_ge(s["scale2_ready"], b + 1)
                for t in range(NT):
                    ins = V.tensor_scalar(xn[:, t, :], xo[:, t, :], mv2[:, t, 0:1], ss2[:, 1, t:t + 1], ALU.subtract, ALU.mult)
                ins.then_inc(s["xn_ready"], 1)
                for t in range(NT):
                    ins = V.tensor_scalar(h2_all[:, one(b, t), :], xo[:, t, :].unsqueeze(1), mv2[:, t, 0:1], ss2[:, 0, t:t + 1], ALU.subtract, ALU.mult)
                link(ins)
                assert link.n == PER_FRONT, link.n

            def rotate_keys(b):
                link = Chain(dve, "chain_keys", 3, b)
                dve.wait_ge(s["k_lat"], 2 * b + 2)
                kr = wm[1][:, 0:NT * KD].rearrange("p (t d) -> p t d", t=NT)[:, :, R:KD].rearrange("p t (e d) -> p t e d", e=2)
                V.tensor_tensor(kt1[:], kr, rope_cs[:, :, 0:1, :].to_broadcast([P, NT, 2, HALF]), ALU.mult)
                V.tensor_tensor(kt2[:, :, 0, :], kr[:, :, 1, :], rope_cs[:, :, 1, :], ALU.mult)
                link(V.tensor_tensor(kt2[:, :, 1, :], kr[:, :, 0, :], rope_cs[:, :, 2, :], ALU.mult))
                link(V.tensor_tensor(kf[:, :, R:KD], kt1[:].rearrange("p t e d -> p t (e d)"), kt2[:].rearrange("p t e d -> p t (e d)"), ALU.add))
                V.tensor_copy(ks[:, 0, :, 0:KD], kf[:])
                link(V.tensor_copy(ks[:, 0, :, KD:2 * KD], kf[:]))
                V.tensor_tensor(ks[:, 1, :, 0:KD], kf[:], ks[:, 0, :, 0:KD].bitcast(f32), ALU.subtract)
                V.tensor_tensor(ks[:, 1, :, KD:2 * KD], kf[:], ks[:, 0, :, 0:KD].bitcast(f32), ALU.subtract).then_inc(s["k_split"], 1)

            def keys_turn(b):
                wait(dve, "b_psum", NU * b)
                dve.wait_ge(s["kTa_ready"], b + 1)
                V.tensor_copy(kTb[:], kTa[:].bitcast(f32)).then_inc(s["kTb_ready"], 1)

            def latent_turn(b):
                wait(dve, "pv_psum", NT * b)
                dve.wait_ge(s["k_lat"], 2 * b + 2)
                V.tensor_copy(lat1[:, :, 0:R], latn[:]).then_inc(s["lat1_ready"], 1)

            def rotate(b, t):
                dve.wait_ge(s["q_psum"], NT * b + t + 1)
                q = wa[:].rearrange("p (h e d) -> p h e d", h=NH, e=2)
                V.tensor_tensor(q1[:].rearrange("p h e d -> p (h e) d"), q.rearrange("p h e d -> p (h e) d"),
                                rope_cs[:, t, 0:1, :].to_broadcast([P, 2 * NH, HALF]), ALU.mult)
                V.tensor_tensor(q2[:, :, 0, :], q[:, :, 1, :], rope_cs[:, t, 1:2, :].to_broadcast([P, NH, HALF]), ALU.mult)
                V.tensor_tensor(q2[:, :, 1, :], q[:, :, 0, :], rope_cs[:, t, 2:3, :].to_broadcast([P, NH, HALF]), ALU.mult).then_inc(s["q_rope"], 1)

            def maxima(b, t, u):
                per = NI // (t + 1)
                dve.wait_ge(s["a_psum"], unit(b, t, u))
                V.tensor_reduce(mx[:, t, per * u:per * (u + 1)], maxima_bank(t, u)[:].rearrange("p (h k) -> p h k", h=per), op=ALU.max, axis=AX.X).then_inc(s["mx_ready"], 1)

            def normalise(b, t):
                link = Chain(dve, "chain_attn", NT, b)
                link.n = t
                dve.wait_ge(s["zsT_psum"], NT * b + t + 1)
                z = pV[:].rearrange("p (m j l) -> p m j l", m=NI, j=NI)
                link(V.reciprocal(rc[:], z[:, :, :, R:R + 1]))
                V.tensor_tensor(yn[:], z[:, :, :, 0:R], rc[:].to_broadcast([P, NI, NI, R]), ALU.mult).then_inc(s["yn_ready"], 1)

            def add_attention(b, t):
                dve.wait_ge(s["y_psum"], NT * b + t + 1)
                V.tensor_tensor(h2_all[:, one(b, t), :], pV[:, 0:C].unsqueeze(1), h2_all[:, one(b, t), :], ALU.add).then_inc(s["x3_ready"], 1)

            def copied3(b):
                link = expert_chain[0] = Chain(dve, "chain_experts", PER_EXPERTS, b)
                dve.wait_ge(s["x3_ready"], NT * (b + 1))
                V.tensor_copy(x3[:], h2_all[:, tiles(b), :]).then_inc(s["x3_copied"], 1)

            def variance3(b):
                dve.wait_ge(s["ms_ready"], NT * (b + 1))
                V.tensor_scalar(ms[:], ms[:], 1.0 / C, 1e-5, ALU.mult, ALU.add).then_inc(s["var3_ready"], 1)

            def normed3(b):
                dve.wait_ge(s["scale3_ready"], b + 1)
                for t in range(NT):
                    ins = V.tensor_scalar(xn3[:, t, :], x3[:, t, :], r3[:, t:t + 1], None, ALU.mult)
                ins.then_inc(s["xn3_ready"], 1)

            full = [P, NT, NE]

            def two_best(b):
                link = expert_chain[0]
                dve.wait_ge(s["lg_psum"], b + 1)
                link(V.tensor_tensor(logits[:], wm[0][:, 0:NT * NE].rearrange("p (t e) -> p t e", t=NT), ebias[:].unsqueeze(1).to_broadcast(full), ALU.add))
                dve.sem_inc(s["dve_passed"], 1)
                for t in range(NT):
                    ins = V.max(best[:, t, :], logits[:, t, :])
                link(ins)
                V.tensor_tensor(dm[:], best[:, :, 1:2], best[:, :, 0:1], ALU.subtract)
                dve.sem_inc(s["dve_passed"], 1)
                for t in range(NT):
                    ins = V.max_index(besti[:, t, :], best[:, t, :], logits[:, t, :])
                ins.then_inc(s["dm_ready"], 1)

            def hot(b):
                link = expert_chain[0]
                dve.wait_ge(s["dm_ready"], b + 1)
                link(V.tensor_copy(bestf[:, :, 0:2], besti[:, :, 0:2]))
                V.tensor_tensor(oh1[:], number.unsqueeze(1).to_broadcast(full), bestf[:, :, 0:1].to_broadcast(full), ALU.is_equal)
                link(V.tensor_tensor(oh2[:], number.unsqueeze(1).to_broadcast(full), bestf[:, :, 1:2].to_broadcast(full), ALU.is_equal))

            def combine_weights(b):
                link = expert_chain[0]
                dve.wait_ge(s["e2_ready"], b + 1)
                link(V.tensor_scalar(p1[:], e2[:], 1.0, 2.0, ALU.add, ALU.mult))
                for t in range(NT):
                    V.scalar_tensor_tensor(out=oh[:, t, :], in0=oh2[:, t, :], scalar=e2[:, t, :], in1=oh1[:, t, :], op0=ALU.mult, op1=ALU.add)
                link(V.reciprocal(p1[:], p1[:]))
                link(V.tensor_tensor(comb[:], oh[:], p1[:].to_broadcast(full), ALU.mult))
                link(V.tensor_copy(comb2[:, :, 0, :], comb[:]))
                V.tensor_tensor(comb2[:, :, 1, :], comb[:], comb2[:, :, 0, :].bitcast(f32), ALU.subtract).then_inc(s["comb_ready"], 1)

            def inner(b, p):
                link = expert_chain[0]
                rows = P if p < NP else EI
                w = wm[(p + 1) % 2]
                dve.wait_ge(s["th_ready"], (NP + 1) * b + p + 1)
                link(V.scalar_tensor_tensor(out=s1[0:rows, p, :], in0=th[0:rows, p, :], scalar=1.0, in1=w[0:rows, 0:S], op0=ALU.add, op1=ALU.mult))
                if p < NP:
                    V.tensor_tensor(s1[:, p, :], s1[:, p, :], w[:, S:2 * S], ALU.mult).then_inc(s["gu_read"], 1)
                else:
                    V.scalar_tensor_tensor(out=hid[0:EI, p, :], in0=s1[0:EI, p, :], scalar=0.5, in1=w[EI:2 * EI, 0:S], op0=ALU.mult, op1=ALU.mult).then_inc(s["gu_read"], 1)

            def weigh(b):
                dve.wait_ge(s["gu_read"], (NP + 1) * (b + 1))
                for a in range(2):
                    dve.wait_ge(s["combB_psum"], 2 * b + a + 1)
                    V.tensor_tensor(hid[:, 2 * a:2 * a + 2, :], s1[:, 2 * a:2 * a + 2, :], wm[a][:].rearrange("p (e s) -> p e s", e=2), ALU.mult).then_inc(s["hid_ready"], 1)

            def finish(b):
                link = expert_chain[0]
                dve.wait_ge(s["moe_psum"], b + 1)
                V.tensor_tensor(flat(fin[:]), wm[0][:, 0:S], flat(x3[:]), ALU.add).then_inc(s["moe_read"], 1)
                dve.wait_ge(s["moe_read"], b + 2)
                dve.wait_ge(s["x_kept"], b + 1)
                dve.wait_ge(s["out_done"], 16 * (b + 1))
                link(V.scalar_tensor_tensor(out=outt[:], in0=fin[:], scalar=tgf[:, 0:1], in1=x_all[:, tiles(b), :], op0=ALU.mult, op1=ALU.add))
                dve.sem_inc(s["out_ready"], 1)
                assert link.n == PER_EXPERTS, link.n

            def round_(i):
                setup, front, queries, weights, experts = has(i)
                if weights:
                    keys_turn(i)
                    maxima(i, 1, 0)
                if front:
                    norms(i + 2)
                if weights:
                    maxima(i, 1, 1)
                    latent_turn(i)
                    maxima(i, 1, 2)
                if front:
                    scaled(i + 2)
                if weights:
                    maxima(i, 1, 3)
                if experts:
                    normalise(i - 1, 1)
                if queries:
                    rotate(i + 1, 0)
                    rotate_keys(i + 1)
                if experts:
                    add_attention(i - 1, 1)
                if weights:
                    maxima(i, 1, 4)
                if experts:
                    copied3(i - 1)
                if weights:
                    maxima(i, 1, 5)
                if front:
                    x_max(i + 2, 1)
                if setup:
                    gate_bias()
                if experts:
                    variance3(i - 1)
                if setup:
                    value_blocks()
                if weights:
                    maxima(i, 1, 6)
                    maxima(i, 1, 7)
                if experts:
                    normed3(i - 1)
                if front:
                    x_max(i + 2, 0)
                if experts:
                    two_best(i - 1)
                    inner(i - 1, 0)
                    hot(i - 1)
                if queries:
                    maxima(i + 1, 0, 0)
                if experts:
                    inner(i - 1, 1)
                    inner(i - 1, 2)
                    combine_weights(i - 1)
                    inner(i - 1, 3)
                if queries:
                    maxima(i + 1, 0, 1)
                if experts:
                    inner(i - 1, 4)
                if queries:
                    rotate(i + 1, 1)
                if weights:
                    normalise(i, 0)
                if queries:
                    maxima(i + 1, 0, 2)
                if setup:
                    split_rope_weights()
                    split_nope_weights()
                    split_expert_weights()
                if experts:
                    weigh(i - 1)
                if front:
                    mix(i + 2)
                if queries:
                    maxima(i + 1, 0, 3)
                if front:
                    norms2(i + 2)
                if experts:
                    finish(i - 1)
                if weights:
                    add_attention(i, 0)
                if front:
                    normed(i + 2)

            schedule(dve, round_)


_INS = ["x", "ctx_1024", "g_xattn", "g_ffn"] + ["L0_xattn_" + n for n in ("q_w", "k_w", "norm_w", "gate_w", "gate_b")] + \
    ["L0_ffn_" + n for n in ("w_ln1", "Wq", "Wkva", "Wkvb", "Wo", "w_ln2", "Wgate", "expert_bias", "Wg", "Wu", "Wd", "sWg", "sWu", "sWd")]


def constants():
    freqs = (np.float32(1.0) / np.float32(100000.0) ** (np.arange(0, ROPE, 2, dtype=np.float32) / np.float32(ROPE))).astype(np.float32)
    ang = np.outer(np.arange(S, dtype=np.float32), freqs).astype(np.float32)
    cos, sin = np.cos(ang), np.sin(ang)
    rope = np.stack([cos, -sin, sin], axis=1).reshape(NT, P, 3, HALF).transpose(1, 0, 2, 3)
    k = np.arange(P)
    sel = np.zeros((2 * NE, NP, P), np.float32)
    for e in range(NE):
        sel[[e, NE + e], e // 2, EI * (e % 2):EI * (e % 2 + 1)] = 1.0
    mask = np.where(k[None, :] > k[:, None], np.float32(NEG), np.float32(0.0))
    experts = np.tile(np.arange(NE, dtype=np.float32), (P, 1))
    consts = np.concatenate([np.eye(P, dtype=np.float32), mask, rope.astype(np.float32).reshape(P, -1), experts], axis=1)
    return {"c_consts": np.ascontiguousarray(consts, dtype=np.float32), "c_sel": sel}


def kernel(**inputs):
    import concourse.bacc as _bacc
    from concourse.bass_utils import run_bass_kernel_spmd as _run

    nc = _bacc.Bacc("TRN2", target_bir_lowering=False, num_devices=1)
    arrays, aps = {}, {}
    for name, a in [(n, inputs[n]) for n in _INS] + list(constants().items()):
        a = np.ascontiguousarray(a)
        arrays[f"in_{name}"] = a
        aps[name] = nc.dram_tensor(f"in_{name}", a.shape, mybir.dt.from_np(a.dtype), kind="ExternalInput").ap()
    out = nc.dram_tensor("out", (B, S, C), mybir.dt.float32, kind="ExternalOutput").ap()
    build(nc, aps, out)
    r = _run(nc, [arrays], core_ids=[0])
    return r.results[0]["out"]
```
